# Optimizing a Trainium2 kernel written in Bass

```python
import numpy as np
import jax
import jax.numpy as jnp

def _softmax(x, axis=-1):
    return jax.nn.softmax(x, axis=axis)

def _gelu(x):
    return jax.nn.gelu(x, approximate=True)

def _silu(x):
    return jax.nn.silu(x)

def _sigmoid(x):
    return jax.nn.sigmoid(x)

def _layernorm(x, axis=-1, eps=1e-05):
    m = jnp.mean(x, axis=axis, keepdims=True)
    v = jnp.var(x, axis=axis, keepdims=True)
    return (x - m) / jnp.sqrt(v + eps)

def _scatter_add(tgt, idx, src, axis=0):
    return tgt.at[idx].add(src)

def _segment_sum(src, seg, n):
    return jax.ops.segment_sum(src, seg, n)
kernel_name = 'mk_xattn_seq_d1_seqx_r4_edb9d5'

def setup_inputs(seed: int=0):
    np.random.seed(seed)
    _w = jnp.asarray

    def _rec_inputs():
        import jax
        import jax.numpy as jnp
        _rk = jax.random.key(seed)
        x = 7.22e-05 + 1 * jax.random.normal(jax.random.fold_in(_rk, 1), (8, 256, 256), jnp.float32)
        _lenS = 256 - jax.random.randint(jax.random.fold_in(_rk, 7), (8,), 0, max(1, 256 // 4) + 1, jnp.int32)
        _lenS2 = 256 - jax.random.randint(jax.random.fold_in(_rk, 8), (8,), 0, max(1, 256 // 4) + 1, jnp.int32)
        _ctx_1024P = jax.random.normal(jax.random.fold_in(_rk, 11), (8, 16, 256), jnp.float32)
        _ctx_1024c = jax.random.dirichlet(jax.random.fold_in(_rk, 511), 0.3 * jnp.ones((16,), jnp.float32), (8, 256))
        _ctx_1024t = jnp.einsum('bsk,bkd->bsd', _ctx_1024c, _ctx_1024P)
        _ctx_1024t = _ctx_1024t * jax.lax.rsqrt(jnp.mean(jnp.square(_ctx_1024t)) + 1e-12) * 0.953939
        ctx_1024 = 4.13588e-05 + 0.999923 * (_ctx_1024t + 0.3 * jax.random.normal(jax.random.fold_in(_rk, 611), (8, 256, 256), jnp.float32))
        _validS = jnp.arange(256)[None, :] < _lenS[:, None]
        _validS2 = jnp.arange(256)[None, :] < _lenS2[:, None]
        _causal = jnp.tril(jnp.ones((256, 256), dtype=bool))
        mask_BxSxS2_fk0 = jnp.where(jnp.broadcast_to(_validS2[:, None, :], (8, 256, 256)), 0.0, 1.0).astype(jnp.float32)
        return (x, ctx_1024, mask_BxSxS2_fk0)
    x, ctx_1024, mask_BxSxS2_fk0 = _rec_inputs()

    def _L0_xattn_setup():
        import jax, jax.numpy as jnp
        import numpy as np
        import math
        B, S, D, H, FF = (4, 512, 256, 16, 1024)
        HD = D // H
        EPS = 1e-05

        def _layer_norm(x, g, b):
            m = jnp.mean(x, axis=-1, keepdims=True)
            v = jnp.mean((x - m) ** 2, axis=-1, keepdims=True)
            return (x - m) * jax.lax.rsqrt(v + EPS) * g + b

        def _self_attn(x, mask, Wq, bq, Wk, bk, Wv, bv, Wo, bo):
            b, s, d = x.shape
            q = (x @ Wq.T + bq).reshape(b, s, H, HD)
            k = (x @ Wk.T + bk).reshape(b, s, H, HD)
            v = (x @ Wv.T + bv).reshape(b, s, H, HD)
            score = jnp.einsum('bshd,bthd->bhst', q, k) / math.sqrt(HD)
            score = score + (1.0 - mask[:, None, :, :]) * -1000000000.0
            p = jax.nn.softmax(score, axis=-1)
            o = jnp.einsum('bhst,bthd->bshd', p, v).reshape(b, s, d)
            return o @ Wo.T + bo
        key = jax.random.key(seed)
        ks = jax.random.split(key, 16)
        sd = 0.02
        inp = {'tgt': jax.random.normal(ks[0], (B, S, D), jnp.float32), 'memory': jax.random.normal(ks[1], (B, S, D), jnp.float32), 'mask': jnp.broadcast_to(jnp.tril(jnp.ones((S, S), jnp.float32)), (B, S, S)), 'Wq': jax.random.normal(ks[2], (D, D), jnp.float32) * sd, 'bq': jnp.zeros((D,), jnp.float32), 'Wk': jax.random.normal(ks[3], (D, D), jnp.float32) * sd, 'bk': jnp.zeros((D,), jnp.float32), 'Wv': jax.random.normal(ks[4], (D, D), jnp.float32) * sd, 'bv': jnp.zeros((D,), jnp.float32), 'Wo': jax.random.normal(ks[5], (D, D), jnp.float32) * sd, 'bo': jnp.zeros((D,), jnp.float32), 'Wg': jax.random.normal(ks[6], (D, D), jnp.float32) * sd, 'bg': jnp.zeros((D,), jnp.float32), 'W1': jax.random.normal(ks[7], (FF, D), jnp.float32) * sd, 'b1': jnp.zeros((FF,), jnp.float32), 'W2': jax.random.normal(ks[8], (D, FF), jnp.float32) * sd, 'b2': jnp.zeros((D,), jnp.float32), 'g1': jnp.ones((D,), jnp.float32), 'be1': jnp.zeros((D,), jnp.float32), 'g2': jnp.ones((D,), jnp.float32), 'be2': jnp.zeros((D,), jnp.float32)}
        return inp
    _L0_xattn_all = _L0_xattn_setup()
    _L0_xattn_in = {k: v for k, v in _L0_xattn_all.items() if k in ('Wq', 'bq', 'Wk', 'bk', 'Wv', 'bv', 'Wo', 'bo', 'Wg', 'bg', 'W1', 'b1', 'W2', 'b2', 'g1', 'be1', 'g2', 'be2')}
    del _L0_xattn_all
    return {'x': x, 'ctx_1024': ctx_1024, 'mask_BxSxS2_fk0': mask_BxSxS2_fk0, 'L0_xattn_Wq': _L0_xattn_in['Wq'], 'L0_xattn_bq': _L0_xattn_in['bq'], 'L0_xattn_Wk': _L0_xattn_in['Wk'], 'L0_xattn_bk': _L0_xattn_in['bk'], 'L0_xattn_Wv': _L0_xattn_in['Wv'], 'L0_xattn_bv': _L0_xattn_in['bv'], 'L0_xattn_Wo': _L0_xattn_in['Wo'], 'L0_xattn_bo': _L0_xattn_in['bo'], 'L0_xattn_Wg': _L0_xattn_in['Wg'], 'L0_xattn_bg': _L0_xattn_in['bg'], 'L0_xattn_W1': _L0_xattn_in['W1'], 'L0_xattn_b1': _L0_xattn_in['b1'], 'L0_xattn_W2': _L0_xattn_in['W2'], 'L0_xattn_b2': _L0_xattn_in['b2'], 'L0_xattn_g1': _L0_xattn_in['g1'], 'L0_xattn_be1': _L0_xattn_in['be1'], 'L0_xattn_g2': _L0_xattn_in['g2'], 'L0_xattn_be2': _L0_xattn_in['be2']}

def reference(x, ctx_1024, mask_BxSxS2_fk0, L0_xattn_Wq, L0_xattn_bq, L0_xattn_Wk, L0_xattn_bk, L0_xattn_Wv, L0_xattn_bv, L0_xattn_Wo, L0_xattn_bo, L0_xattn_Wg, L0_xattn_bg, L0_xattn_W1, L0_xattn_b1, L0_xattn_W2, L0_xattn_b2, L0_xattn_g1, L0_xattn_be1, L0_xattn_g2, L0_xattn_be2):
    import jax
    import jax.numpy as jnp

    def _L0_xattn_ref(tgt, memory, mask, Wq, bq, Wk, bk, Wv, bv, Wo, bo, Wg, bg, W1, b1, W2, b2, g1, be1, g2, be2):
        import jax, jax.numpy as jnp
        import numpy as np
        import math
        B, S, D, H, FF = (4, 512, 256, 16, 1024)
        HD = D // H
        EPS = 1e-05

        def _layer_norm(x, g, b):
            m = jnp.mean(x, axis=-1, keepdims=True)
            v = jnp.mean((x - m) ** 2, axis=-1, keepdims=True)
            return (x - m) * jax.lax.rsqrt(v + EPS) * g + b

        def _self_attn(x, mask, Wq, bq, Wk, bk, Wv, bv, Wo, bo):
            b, s, d = x.shape
            q = (x @ Wq.T + bq).reshape(b, s, H, HD)
            k = (x @ Wk.T + bk).reshape(b, s, H, HD)
            v = (x @ Wv.T + bv).reshape(b, s, H, HD)
            score = jnp.einsum('bshd,bthd->bhst', q, k) / math.sqrt(HD)
            score = score + (1.0 - mask[:, None, :, :]) * -1000000000.0
            p = jax.nn.softmax(score, axis=-1)
            o = jnp.einsum('bhst,bthd->bshd', p, v).reshape(b, s, d)
            return o @ Wo.T + bo
        tgt1 = _layer_norm(tgt, g1, be1)
        tgt = tgt + _self_attn(tgt1, mask, Wq, bq, Wk, bk, Wv, bv, Wo, bo)
        tgt = tgt + (memory @ Wg.T + bg)
        tgt1 = _layer_norm(tgt, g2, be2)
        ff = jax.nn.relu(tgt1 @ W1.T + b1) @ W2.T + b2
        return tgt + ff
    x = _L0_xattn_ref(x, ctx_1024, mask_BxSxS2_fk0, L0_xattn_Wq, L0_xattn_bq, L0_xattn_Wk, L0_xattn_bk, L0_xattn_Wv, L0_xattn_bv, L0_xattn_Wo, L0_xattn_bo, L0_xattn_Wg, L0_xattn_bg, L0_xattn_W1, L0_xattn_b1, L0_xattn_W2, L0_xattn_b2, L0_xattn_g1, L0_xattn_be1, L0_xattn_g2, L0_xattn_be2)
    return x

_drawn_inputs = setup_inputs


def setup_inputs(seed=0):
    import zlib

    import numpy as np

    out = dict(_drawn_inputs(seed))
    spreads = {'L0_xattn_bq': (0.0, 0.8),
     'L0_xattn_bk': (0.0, 0.8),
     'L0_xattn_bv': (0.0, 0.1),
     'L0_xattn_bo': (0.0, 0.1),
     'L0_xattn_bg': (0.0, 0.1),
     'L0_xattn_b1': (0.0, 0.1),
     'L0_xattn_b2': (0.0, 0.1),
     'L0_xattn_g1': (1.0, 0.6),
     'L0_xattn_be1': (0.0, 0.8),
     'L0_xattn_g2': (1.0, 0.6),
     'L0_xattn_be2': (0.0, 0.592)}
    factors = {'L0_xattn_Wq': 8.0, 'L0_xattn_Wk': 8.0}
    for name, (base, spread) in spreads.items():
        noise = np.random.default_rng([zlib.crc32(name.encode()), seed]).standard_normal(out[name].shape)
        drawn = base * np.exp(spread * noise) if base else spread * noise
        out[name] = jnp.asarray(drawn.astype(out[name].dtype))
    for name, factor in factors.items():
        out[name] = (out[name] * factor).astype(out[name].dtype)
    return out
```

```python
from contextlib import ExitStack

import concourse.bass as bass
from concourse import mybir

F32 = mybir.dt.float32
F16 = mybir.dt.float16
BF16 = mybir.dt.bfloat16
ALU = mybir.AluOpType
ACT = mybir.ActivationFunctionType

P = 128
BATCHES, S, D = 8, 256, 256
HEADS = 16
HD = D // HEADS
FF = 1024
NT = S // P
NK = D // P
NF = FF // P
UNITS = NF // 2
EPS = 1e-5
MASKED = 1e9
LOWEST = -3.4e38
SCALE = HD ** -0.5

GROUP = 4
GROUPS = HEADS // GROUP
COLS = P // GROUP
T_LAG = 2
SM_RING = 4
PT_RING = 8
PARTS = 2
STACK = 80

Q_PARTS = (0, 0, 1, 1)
K_PARTS = (0, 1, 0, 1)

C_G1, C_BE1, C_B, C_G2, C_BE2, C_B1 = 0, 2, 4, 10, 12, 14
N_COLS = 22
WQ, WK, WV, WO, WG = range(5)

SLOT_CTX = 0
SLOT_OT = (1, 3)
SLOT_ON = 5
SLOT_XT = 6
SLOT_PROJ = 7
SLOT_Q = 8
SLOT_K = 9
SLOT_L2T = 10
SLOT_F1 = (11, 12, 13, 14)
SLOT_F2 = {14: (0, 1), 15: (2, 3)}
SLOT_V = 15
SLOT_LN1 = 3


def build(nc, x, ctxT, mask, wqT, wkT, wvT, woT, wgT, w1T, w2T, cols, rows, eye, out):
    x_t, mask_t, ctx_t, out_t = (v.rearrange("(j e) (t p) d -> j e p t d", e=2, p=P) for v in (x, mask, ctxT, out))
    scratch = nc.dram_tensor("qk_scratch", [2, 2, PARTS, D, S], F16, kind="Internal").ap()

    with ExitStack() as stack:
        def sb(name, shape, dt=F32):
            return stack.enter_context(nc.sbuf_tensor(name, shape, dt))

        def bank(name):
            return stack.enter_context(nc.psum_tensor(name, [P, 512], F32))

        def sem(name):
            return stack.enter_context(nc.semaphore(name))

        w_raw = sb("w_raw", [P, 5, NK, D])
        w1_raw = sb("w1_raw", [P, NK, FF])
        w2_raw = sb("w2_raw", [P, NF, D])
        w_scaled = sb("w_scaled", [P, 3, NK, D])
        w1_scaled = sb("w1_scaled", [P, NK, FF])
        w_hi = sb("w_hi", [P, 5, NK, D], F16)
        w_lo = sb("w_lo", [P, 5, NK, D], BF16)
        w1_hi = sb("w1_hi", [P, NK, FF], F16)
        w1_lo = sb("w1_lo", [P, NK, FF], BF16)
        w2_hi = sb("w2_hi", [P, NF, D], F16)
        w2_lo = sb("w2_lo", [P, NF, D], BF16)
        col = sb("col", [P, N_COLS])
        row = sb("row", [P, 3, D])
        ident = sb("ident", [P, P])
        bias_qkv = sb("bias_qkv", [P, 6])
        bias_q = sb("bias_q", [P, 2])
        bias_h = sb("bias_h", [P, NF])
        bv_wide = sb("bv_wide", [P, NK, P])
        minus_half = sb("minus_half", [P, NT])
        bog = sb("bog", [P, D])
        bias_t2 = sb("bias_t2", [P, D])

        x_in = [sb(f"x_in{p}", [P, NT, D]) for p in range(2)]
        stats1 = sb("stats1", [P, NT, 6])
        mv1 = sb("mv1", [P, NT, 2])
        var1, rstd1 = sb("var1", [P, NT]), sb("rstd1", [P, NT])
        xn = sb("xn", [P, NT, D])
        xT = [sb(f"xT{q}", [P, NK, S], F16) for q in range(PARTS)]
        qk_parts = sb("qk_parts", [P, 2, PARTS, NK, S], F16)
        q_stack = [sb(f"q_stack{p}", [STACK, HEADS, S], F16) for p in range(2)]
        k_stack = [sb(f"k_stack{p}", [STACK, HEADS, S], F16) for p in range(2)]
        v_cols = [sb(f"v_cols{p}", [P, NT, HEADS, COLS]) for p in range(2)]
        mask_in = [sb(f"mask_in{p}", [P, NT, S]) for p in range(2)]
        mask_bias = [sb(f"mask_bias{p}", [P, NT, S]) for p in range(2)]

        masked = sb("masked", [P, SM_RING, NT, S])
        top = sb("top", [P, SM_RING, NT])
        probsT = sb("probsT", [P, PT_RING, NT, S])

        oT_wide = sb("oT_wide", [P, GROUPS, S])
        recip = sb("recip", [P, NT, HEADS])
        o_norm = sb("o_norm", [P, NT, HEADS, HD])
        oT = [sb(f"oT{q}", [P, NK, S], F16) for q in range(PARTS)]
        ctx_in = [sb(f"ctx_in{p}", [P, NK, S]) for p in range(2)]
        cT = [sb(f"cT{q}", [P, NK, S], F16) for q in range(PARTS)]
        x_res = [sb(f"x_res{p}", [P, NT, D]) for p in range(2)]
        x_bias = sb("x_bias", [P, NT, D])
        t2 = sb("t2", [P, NT, D])
        t2_b2 = sb("t2_b2", [P, NT, D])
        stats2 = sb("stats2", [P, NT, 6])
        mv2 = sb("mv2", [P, NT, 2])
        var2, rstd2 = sb("var2", [P, NT]), sb("rstd2", [P, NT])
        tn = sb("tn", [P, NT, D])
        tT = [sb(f"tT{q}", [P, NK, S], F16) for q in range(PARTS)]
        relu32 = sb("relu32", [P, 2, 2, S])
        hid = [sb(f"hid{q}", [P, NF, S], F16) for q in range(PARTS)]
        y = sb("y", [P, NT, D])

        score_bank = [bank(f"score_bank{n}") for n in range(2)]
        turn_bank = [bank(f"turn_bank{n}") for n in range(2)]
        av_bank = bank("av_bank")
        lin = [bank(f"lin{n}") for n in range(3)]

        def halves(t):
            return t[:, :].rearrange("p (h c) -> p h c", h=2)

        ot_bank = [lin[0], lin[1]]
        on_bank, xt_bank, proj_bank, q_bank, k_bank = lin[2], lin[0], lin[1], lin[2], lin[0]
        l2t_bank, f1_bank, f2_bank, v_bank = lin[1], [lin[2], lin[0], lin[1], lin[2]], lin[0], lin[1]

        cols_in, eye_in, rows_in = sem("cols_in"), sem("eye_in"), sem("rows_in")
        qkv_in, og_in, w1_in, w2_in = sem("qkv_in"), sem("og_in"), sem("w1_in"), sem("w2_in")
        x_loaded = [sem(f"x_loaded{p}") for p in range(2)]
        mask_loaded = [sem(f"mask_loaded{p}") for p in range(2)]
        ctx_loaded = [sem(f"ctx_loaded{p}") for p in range(2)]
        res_loaded = [sem(f"res_loaded{p}") for p in range(2)]
        scratch_written = sem("scratch_written")
        stacked = [sem(f"stacked{p}") for p in range(2)]
        y_free = sem("y_free")
        dve_passed, pool_passed, sp_passed = sem("dve_passed"), sem("pool_passed"), sem("sp_passed")
        w_scaled_done, w_hi_done, w_lo_done = sem("w_scaled_done"), sem("w_hi_done"), sem("w_lo_done")
        wx_hi_done, wx_lo_done, w1_scaled_done = sem("wx_hi_done"), sem("wx_lo_done"), sem("w1_scaled_done")
        bias_mm, bias_done, late_mm, late_done = sem("bias_mm"), sem("bias_done"), sem("late_mm"), sem("late_done")
        zeroed, half_set = sem("zeroed"), sem("half_set")
        st1_done, mv1_done, var1_done = sem("st1_done"), sem("mv1_done"), sem("var1_done")
        rstd1_done, xn_done = sem("rstd1_done"), sem("xn_done")
        xt_ready, xt_hi, xt_split = sem("xt_ready"), sem("xt_hi"), sem("xt_split")
        q_ready, q_hi, q_split = sem("q_ready"), sem("q_hi"), sem("q_split")
        k_ready, k_hi, k_split = sem("k_ready"), sem("k_hi"), sem("k_split")
        v_ready, v_copied = sem("v_ready"), sem("v_copied")
        mask_ready = sem("mask_ready")
        scores_ready, max_done, sub_done = sem("scores_ready"), sem("max_done"), sem("sub_done")
        turned, exp_done, av_ready, av_copied = sem("turned"), sem("exp_done"), sem("av_ready"), sem("av_copied")
        ot_ready, recip_done, o_done = sem("ot_ready"), sem("recip_done"), sem("o_done")
        on_ready, on_hi, on_split = sem("on_ready"), sem("on_hi"), sem("on_split")
        ctx_hi, ctx_split, x_bias_done = sem("ctx_hi"), sem("ctx_split"), sem("x_bias_done")
        proj_ready, t2_done, t2_b2_done = sem("proj_ready"), sem("t2_done"), sem("t2_b2_done")
        st2_done, mv2_done, var2_done = sem("st2_done"), sem("mv2_done"), sem("var2_done")
        rstd2_done, tn_done = sem("rstd2_done"), sem("tn_done")
        l2t_ready, l2t_hi, l2t_split = sem("l2t_ready"), sem("l2t_hi"), sem("l2t_split")
        f1_ready, f1_hi, f1_relu, f1_split = sem("f1_ready"), sem("f1_hi"), sem("f1_relu"), sem("f1_split")
        f2_ready, y_done = sem("f2_ready"), sem("y_done")

        def nth_of_parity(b, p, each):
            return (b - p) * (each // 2) + each

        def run_steps(eng, step):
            step(0, 0, True, False, False)
            step(0, 1, True, True, False)
            with eng.Fori(1, BATCHES // 2) as j:
                step(j, 0, True, True, True)
                step(j, 1, True, True, True)
            step(BATCHES // 2, 0, False, True, True)
            step(BATCHES // 2, 1, False, False, True)

        def batch(tensor, j, p, back):
            return tensor[j + (p - back) // 2, (p - back) % 2]

        def behind(i, h, lag, has_b, has_c):
            return (i - 1, h - lag, has_b) if h >= lag else (i - 2, HEADS + h - lag, has_c)

        block = stack.enter_context(nc.Block())

        @block.sync
        def _(sp):
            sp.dma_start(col[:, :], cols).then_inc(cols_in, 16)
            sp.dma_start(x_in[0][:, :, :], x_t[0, 0]).then_inc(x_loaded[0], 16)
            for n, w in ((WQ, wqT), (WK, wkT), (WV, wvT)):
                sp.dma_start(w_raw[:, n, :, :], w.rearrange("(k p) n -> p k n", p=P)).then_inc(qkv_in, 16)
            sp.dma_start(ident[:, :], eye).then_inc(eye_in, 16)
            for n, w in ((WO, woT), (WG, wgT)):
                sp.dma_start(w_raw[:, n, :, :], w.rearrange("(k p) n -> p k n", p=P)).then_inc(og_in, 16)
            sp.dma_start(row[:, :, :], rows.partition_broadcast(P)).then_inc(rows_in, 16)

            def step(j, p, has_a, has_b, has_c):
                i = 2 * j + p
                q = 1 - p
                if has_a:
                    if not isinstance(i, int) or i >= 2:
                        sp.wait_ge(xn_done, (i - 1) * NT)
                        sp.sem_inc(sp_passed, 1)
                    if not isinstance(i, int) or i >= 1:
                        sp.dma_start(x_in[p][:, :, :], batch(x_t, j, p, 0)).then_inc(x_loaded[p], 16)
                    if not isinstance(i, int) or i >= 2:
                        sp.wait_ge(mask_ready, i - 1)
                        sp.sem_inc(sp_passed, 1)
                    sp.dma_start(mask_in[p][:, :, :], batch(mask_t, j, p, 0)).then_inc(mask_loaded[p], 16)
                if has_b:
                    sp.dma_start(ctx_in[q][:, :, :], batch(ctx_t, j, p, 1)).then_inc(ctx_loaded[q], 16)
                    sp.dma_start(x_res[q][:, :, :], batch(x_t, j, p, 1)).then_inc(res_loaded[q], 16)
                if has_a:
                    if not isinstance(i, int) or i >= 2:
                        sp.wait_ge(stacked[p], nth_of_parity(i - 2, p, 16 * 8))
                        sp.sem_inc(sp_passed, 1)
                        sp.wait_ge(scores_ready, (i - 1) * HEADS)
                        sp.sem_inc(sp_passed, 1)
                    sp.wait_ge(q_split, (i + 1) * NK)
                    sp.sem_inc(sp_passed, 1)
                    sp.dma_start(scratch[p, 0].rearrange("t (k p) s -> p t k s", p=P),
                                 qk_parts[:, 0, :, :, :]).then_inc(scratch_written, 16)
                    sp.wait_ge(k_split, (i + 1) * NK)
                    sp.sem_inc(sp_passed, 1)
                    sp.dma_start(scratch[p, 1].rearrange("t (k p) s -> p t k s", p=P),
                                 qk_parts[:, 1, :, :, :]).then_inc(scratch_written, 16)
                    sp.wait_ge(scratch_written, (i + 1) * 32)
                    sp.sem_inc(sp_passed, 1)
                    for kind, dst, parts in ((0, q_stack[p], Q_PARTS), (1, k_stack[p], K_PARTS)):
                        for n, part in enumerate(parts):
                            sp.dma_start(dst[n * HD:(n + 1) * HD, :, :],
                                         scratch[p, kind, part].rearrange("(h r) s -> r h s", r=HD)
                                         ).then_inc(stacked[p], 16)

            run_steps(sp, step)

        @block.tensor
        def _(pe):
            def turn(dst, src):
                for k in range(2):
                    for t in range(2):
                        last = pe.transpose(dst[:, k, t * P:(t + 1) * P], src[:, t, k * P:(k + 1) * P],
                                            ident[:, :])
                return last

            def product(dst, left, right, start, stop, open_group=False):
                pairs = ((0, 0), (1, 0), (0, 1))
                for n, (a, b) in enumerate(pairs):
                    last = pe.matmul(dst, left[a], right[b], start=start and n == 0,
                                     stop=stop and n == len(pairs) - 1, skip_group_check=open_group)
                return last

            def bias_qkv_products():
                pe.wait_ge(cols_in, 16)
                pe.wait_ge(qkv_in, 48)
                for w in range(3):
                    for m in range(NK):
                        for k in range(NK):
                            last = pe.matmul(lin[1][:, 2 * w + m:2 * w + m + 1],
                                             w_raw[:, w, k, m * P:(m + 1) * P],
                                             col[:, C_BE1 + k:C_BE1 + k + 1], start=k == 0, stop=k == NK - 1)
                last.then_inc(bias_mm, 1)

            def late_bias_products():
                pe.wait_ge(w1_in, 16)
                pe.wait_ge(k_split, NK)
                for m in range(NF):
                    for k in range(NK):
                        last = pe.matmul(lin[0][:, m:m + 1], w1_raw[:, k, m * P:(m + 1) * P],
                                         col[:, C_BE2 + k:C_BE2 + k + 1], start=k == 0, stop=k == NK - 1)
                last.then_inc(late_mm, 1)
                pe.wait_ge(og_in, 32)
                pe.wait_ge(bias_done, 3)
                pe.wait_ge(v_copied, 1)
                for k in range(NK):
                    last = pe.matmul(lin[1][:, 0:D], bv_wide[:, k, :], w_raw[:, WO, k, :],
                                     start=k == 0, stop=k == NK - 1)
                last.then_inc(late_mm, 1)

            def scores(b, h, p):
                if h == 0:
                    pe.wait_ge(stacked[p], nth_of_parity(b, p, 16 * 8))
                if not isinstance(b, int) or b * HEADS + h >= 2:
                    pe.wait_ge(max_done, b * HEADS * NT + (h - 1) * NT)
                for t in range(NT):
                    last = pe.matmul(halves(score_bank[h % 2])[:, t, :], q_stack[p][:, h, t * P:(t + 1) * P],
                                     k_stack[p][:, h, :], start=True, stop=True)
                last.then_inc(scores_ready, 1)

            def turn_scores(b, h):
                pe.wait_ge(sub_done, b * HEADS + h + 1)
                if not isinstance(b, int) or b * HEADS + h >= 2:
                    pe.wait_ge(exp_done, b * HEADS + h - 1)
                turn(halves(turn_bank[h % 2]), masked[:, h % SM_RING, :, :]).then_inc(turned, 1)

            def apply_v(b, g, p):
                if g == 0:
                    pe.wait_ge(v_copied, b + 1)
                pe.wait_ge(exp_done, b * HEADS + (g + 1) * GROUP)
                if not isinstance(b, int) or b * GROUPS + g >= 1:
                    pe.wait_ge(av_copied, b * GROUPS + g)
                for t in range(NT):
                    for j in range(GROUP):
                        h = g * GROUP + j
                        last = pe.matmul(av_bank[j * COLS:(j + 1) * COLS, 0:S], v_cols[p][:, t, h, :],
                                         probsT[:, h % PT_RING, t, :], start=t == 0, stop=t == NT - 1,
                                         skip_group_check=True)
                last.then_inc(av_ready, 1)

            def project(bank_, w):
                for m in range(NK):
                    for k in range(NK):
                        last = product(halves(bank_)[:, m, :],
                                       [t[:, w, k, m * P:(m + 1) * P] for t in (w_hi, w_lo)],
                                       [xT[0][:, k, :], xT[1][:, k, :]], k == 0, k == NK - 1)
                return last

            def step(j, p, has_a, has_b, has_c):
                i = 2 * j + p
                q = 1 - p
                c = i - 2
                more = not isinstance(i, int)
                if isinstance(i, int) and i == 1:
                    pe.wait_ge(late_done, 3)
                    pe.wait_ge(zeroed, 8)
                for h in range(HEADS):
                    if has_b:
                        scores(i - 1, h, q)
                    tb, th, present = behind(i, h, T_LAG, has_b, has_c)
                    if present:
                        turn_scores(tb, th)
                    if h % GROUP == T_LAG % GROUP:
                        tb, th, present = behind(i, h, T_LAG + GROUP, has_b, has_c)
                        if present:
                            apply_v(tb, th // GROUP, q if h >= T_LAG + GROUP else p)
                    if has_c and h in SLOT_OT:
                        u = SLOT_OT.index(h)
                        pe.wait_ge(av_copied, c * GROUPS + 2 * u + 2)
                        if u == 0:
                            if has_b:
                                pe.wait_ge(max_done, (i - 1) * HEADS * NT + NT)
                            else:
                                pe.wait_ge(y_done, c)
                            if more or i <= BATCHES:
                                pe.wait_ge(k_split, (c + 2) * NK)
                        else:
                            if more or i <= BATCHES:
                                pe.wait_ge(v_copied, c + 2)
                        dst = ot_bank[u][:, :].rearrange("p (t g c) -> p t g c", t=NT, g=2)
                        for g in range(2):
                            for t in range(NT):
                                last = pe.transpose(dst[:, t, g, :],
                                                    oT_wide[:, 2 * u + g, t * P:(t + 1) * P], ident[:, :])
                        last.then_inc(ot_ready, 1)
                    if has_c and h == SLOT_ON:
                        pe.wait_ge(o_done, (c + 1) * 2)
                        if more or i <= BATCHES:
                            pe.wait_ge(q_split, (c + 2) * NK)
                        turn(halves(on_bank), o_norm[:, :, :, :].rearrange("p t h d -> p t (h d)")
                             ).then_inc(on_ready, 1)
                    if has_a and h == SLOT_XT:
                        if isinstance(i, int) and i == 0:
                            pe.wait_ge(eye_in, 16)
                        pe.wait_ge(xn_done, (i + 1) * NT)
                        if has_c:
                            pe.wait_ge(o_done, c * 2 + 1)
                        elif i >= 1:
                            pe.wait_ge(k_split, i * NK)
                        turn(halves(xt_bank), xn[:, :, :]).then_inc(xt_ready, 1)
                    if has_c and h == SLOT_PROJ:
                        pe.wait_ge(wx_lo_done, 2)
                        pe.wait_ge(on_split, c + 1)
                        pe.wait_ge(ctx_split, c + 1)
                        pe.wait_ge(o_done, (c + 1) * 2)
                        for t in range(NT):
                            for k in range(NK):
                                for src, w in ((cT, WG), (oT, WO)):
                                    last = product(halves(proj_bank)[:, t, :],
                                                   [s[:, k, t * P:(t + 1) * P] for s in src],
                                                   [w_hi[:, w, k, :], w_lo[:, w, k, :]],
                                                   k == 0 and w == WG, k == NK - 1 and w == WO)
                        last.then_inc(proj_ready, 1)
                    if has_a and h == SLOT_Q:
                        if isinstance(i, int) and i == 0:
                            pe.wait_ge(w_lo_done, 3)
                        pe.wait_ge(xt_split, i + 1)
                        if has_c:
                            pe.wait_ge(on_split, c + 1)
                        elif i >= 1:
                            pe.wait_ge(q_split, i * NK)
                        project(q_bank, WQ).then_inc(q_ready, 1)
                    if has_a and h == SLOT_K:
                        pe.wait_ge(xt_split, i + 1)
                        project(k_bank, WK).then_inc(k_ready, 1)
                    if has_c and h == SLOT_L2T:
                        pe.wait_ge(tn_done, (c + 1) * NT)
                        pe.wait_ge(t2_done, c + 1)
                        turn(halves(l2t_bank), tn[:, :, :]).then_inc(l2t_ready, 1)
                    if has_c and h in SLOT_F1:
                        u = SLOT_F1.index(h)
                        if u == 0:
                            pe.wait_ge(wx_lo_done, 4)
                            pe.wait_ge(l2t_split, c + 1)
                            if has_a:
                                pe.wait_ge(q_split, (i + 1) * NK)
                            else:
                                pe.wait_ge(on_split, c + 1)
                        if u == 1:
                            if has_a:
                                pe.wait_ge(k_split, (i + 1) * NK)
                            else:
                                pe.wait_ge(o_done, (c + 1) * 2)
                        if u == 2:
                            pe.wait_ge(l2t_split, c + 1)
                        if u == 3:
                            pe.wait_ge(f1_relu, c * NF + 2)
                        for half in range(2):
                            m = 2 * u + half
                            for k in range(NK):
                                last = product(halves(f1_bank[u])[:, half, :],
                                               [w[:, k, m * P:(m + 1) * P] for w in (w1_hi, w1_lo)],
                                               [tT[0][:, k, :], tT[1][:, k, :]], k == 0, k == NK - 1)
                        last.then_inc(f1_ready, 1)
                    if has_c and h in SLOT_F2:
                        for u in SLOT_F2[h]:
                            pe.wait_ge(f1_split, c * UNITS + u + 1)
                            if u == 0:
                                pe.wait_ge(f1_relu, c * NF + 4)
                            for t in range(NT):
                                for k in (2 * u, 2 * u + 1):
                                    last = product(halves(f2_bank)[:, t, :],
                                                   [z[:, k, t * P:(t + 1) * P] for z in hid],
                                                   [w2_hi[:, k, :], w2_lo[:, k, :]],
                                                   k == 0 and t == 0, k == NF - 1, open_group=True)
                            if u == UNITS - 1:
                                last.then_inc(f2_ready, 1)
                    if has_a and h == SLOT_V:
                        if has_c:
                            pe.wait_ge(f1_relu, c * NF + 6)
                        elif i >= 1:
                            pe.wait_ge(v_copied, i)
                        else:
                            pe.wait_ge(bias_done, 1)
                        for t in range(NT):
                            for k in range(NK):
                                last = product(halves(v_bank)[:, t, :],
                                               [z[:, k, t * P:(t + 1) * P] for z in xT],
                                               [w_hi[:, WV, k, :], w_lo[:, WV, k, :]], k == 0, k == NK - 1)
                        last.then_inc(v_ready, 1)
                if isinstance(i, int) and i == 0:
                    late_bias_products()

            bias_qkv_products()
            run_steps(pe, step)

        @block.scalar
        def _(act):
            act.sem_inc(y_free, 16)
            act.dma_start(w1_raw[:, :, :], w1T.rearrange("(k p) n -> p k n", p=P)).then_inc(w1_in, 16)
            act.dma_start(w2_raw[:, :, :], w2T.rearrange("(k p) n -> p k n", p=P)).then_inc(w2_in, 16)
            for w in range(3):
                act.wait_ge(w_scaled_done, (w + 1) * NK)
                act.copy(w_hi[:, w, :, :], w_scaled[:, w, :, :]).then_inc(w_hi_done, 1)

            def late_weights():
                act.wait_ge(og_in, 32)
                for w in (WO, WG):
                    act.copy(w_hi[:, w, :, :], w_raw[:, w, :, :]).then_inc(wx_hi_done, 1)
                act.wait_ge(w1_scaled_done, NK)
                act.copy(w1_hi[:, :, :], w1_scaled[:, :, :]).then_inc(wx_hi_done, 1)
                act.wait_ge(w2_in, 16)
                act.copy(w2_hi[:, :, :], w2_raw[:, :, :]).then_inc(wx_hi_done, 1)

            def step(j, p, has_a, has_b, has_c):
                i = 2 * j + p
                c = i - 2
                for h in range(HEADS):
                    tb, th, present = behind(i, h, T_LAG, has_b, has_c)
                    if present:
                        act.wait_ge(turned, tb * HEADS + th + 1)
                        if not isinstance(tb, int) or tb * HEADS + th >= PT_RING:
                            act.wait_ge(av_ready, tb * GROUPS + th // GROUP - 1)
                        act.activation(probsT[:, th % PT_RING, :, :], halves(turn_bank[th % 2]),
                                       ACT.Exp).then_inc(exp_done, 1)
                    if h % GROUP == T_LAG % GROUP:
                        tb, th, present = behind(i, h, T_LAG + GROUP, has_b, has_c)
                        if present:
                            g = th // GROUP
                            act.wait_ge(av_ready, tb * GROUPS + g + 1)
                            act.copy(oT_wide[:, g, :], av_bank[:, 0:S]).then_inc(av_copied, 1)
                    if has_c and h == SLOT_CTX:
                        act.wait_ge(ctx_loaded[p], nth_of_parity(c, p, 16))
                        act.copy(cT[0][:, :, :], ctx_in[p][:, :, :]).then_inc(ctx_hi, 1)
                    if has_c and h == SLOT_ON:
                        act.wait_ge(on_ready, c + 1)
                        act.copy(oT[0][:, :, :], halves(on_bank)).then_inc(on_hi, 1)
                    if has_a and h == SLOT_XT:
                        act.wait_ge(xt_ready, i + 1)
                        act.copy(xT[0][:, :, :], halves(xt_bank)).then_inc(xt_hi, 1)
                    for slot, kind, ready, bank_, hi in ((SLOT_Q, 0, q_ready, q_bank, q_hi),
                                                         (SLOT_K, 1, k_ready, k_bank, k_hi)):
                        if has_a and h == slot:
                            act.wait_ge(ready, i + 1)
                            if isinstance(i, int) and i == 0:
                                act.wait_ge(bias_done, 2)
                            act.wait_ge(scratch_written, i * 32)
                            for m in range(NK):
                                bias = (bias_q[:, m:m + 1], bias_qkv[:, NK + m:NK + m + 1])[kind]
                                act.activation(qk_parts[:, kind, 0, m, :], halves(bank_)[:, m, :],
                                               ACT.Identity, bias=bias).then_inc(hi, 1)
                    if has_c and h == SLOT_L2T:
                        act.wait_ge(l2t_ready, c + 1)
                        act.copy(tT[0][:, :, :], halves(l2t_bank)).then_inc(l2t_hi, 1)
                    if has_c and h in SLOT_F1:
                        u = SLOT_F1.index(h)
                        act.wait_ge(f1_ready, c * UNITS + u + 1)
                        for half in range(2):
                            m = 2 * u + half
                            act.activation(hid[0][:, m, :], halves(f1_bank[u])[:, half, :], ACT.Relu,
                                           bias=bias_h[:, m:m + 1]).then_inc(f1_hi, 1)
                    if has_a and h == SLOT_V:
                        act.wait_ge(v_ready, i + 1)
                        if isinstance(i, int) and i < 2:
                            act.wait_ge(zeroed, 4)
                        act.copy(v_cols[p][:, :, :, 0:HD],
                                 halves(v_bank).rearrange("p t (h d) -> p t h d", d=HD)).then_inc(v_copied, 1)
                if isinstance(i, int) and i == 0:
                    late_weights()
                if isinstance(i, int) and i == 1:
                    act.wait_ge(late_done, 1)
                if has_c:
                    act.wait_ge(y_done, c + 1)
                    act.dma_start(batch(out_t, j, p, 2), y[:, :, :]).then_inc(y_free, 16)

            run_steps(act, step)
            act.wait_ge(y_free, (BATCHES + 1) * 16)

        @block.vector
        def _(dve):
            def moments(src, stats, mv, var, sems, b):
                st_done, mv_done, var_done = sems
                for t in range(NT):
                    dve.bn_stats(stats[:, t, :], src[:, t, :]).then_inc(st_done, 1)
                for t in range(NT):
                    dve.wait_ge(st_done, b * NT + t + 1)
                    dve.sem_inc(dve_passed, 1)
                    dve.bn_aggr(mv[:, t, :], stats[:, t, :]).then_inc(mv_done, 1)
                dve.wait_ge(mv_done, (b + 1) * NT)
                dve.tensor_scalar(var[:, :], mv[:, :, 1], EPS, None, ALU.add).then_inc(var_done, 1)

            def normalize(src, mv, rstd, dst, rstd_done, done, b):
                dve.wait_ge(rstd_done, b + 1)
                for t in range(NT):
                    dve.tensor_scalar(dst[:, t, :], src[:, t, :], mv[:, t, 0:1], rstd[:, t:t + 1],
                                      ALU.subtract, ALU.mult).then_inc(done, 1)

            dve.wait_ge(cols_in, 16)
            dve.wait_ge(qkv_in, 48)
            for w in range(3):
                for k in range(NK):
                    gain = col[:, C_G1 + k:C_G1 + k + 1]
                    dve.tensor_scalar(w_scaled[:, w, k, :], w_raw[:, w, k, :], gain,
                                      SCALE if w == WQ else 1.0, ALU.mult, ALU.mult).then_inc(w_scaled_done, 1)
            dve.wait_ge(x_loaded[0], 16)
            moments(x_in[0], stats1, mv1, var1, (st1_done, mv1_done, var1_done), 0)
            normalize(x_in[0], mv1, rstd1, xn, rstd1_done, xn_done, 0)
            for w in range(3):
                dve.wait_ge(w_hi_done, w + 1)
                dve.tensor_tensor(w_lo[:, w, :, :], w_scaled[:, w, :, :], w_hi[:, w, :, :],
                                  ALU.subtract).then_inc(w_lo_done, 1)
            dve.wait_ge(bias_mm, 1)
            dve.tensor_tensor(bias_qkv[:, :], lin[1][:, 0:6], col[:, C_B:C_B + 6], ALU.add).then_inc(bias_done, 1)
            dve.wait_ge(bias_done, 1)
            dve.tensor_scalar(bias_q[:, :], bias_qkv[:, 0:2], SCALE, None, ALU.mult).then_inc(bias_done, 1)
            dve.tensor_copy(bv_wide[:, :, :], bias_qkv[:, 4:6].unsqueeze(2).to_broadcast([P, NK, P])
                            ).then_inc(bias_done, 1)

            def late_setup():
                dve.wait_ge(w1_in, 16)
                for k in range(NK):
                    dve.tensor_scalar(w1_scaled[:, k, :], w1_raw[:, k, :], col[:, C_G2 + k:C_G2 + k + 1],
                                      None, ALU.mult).then_inc(w1_scaled_done, 1)
                dve.wait_ge(late_mm, 1)
                dve.tensor_tensor(bias_h[:, :], lin[0][:, 0:NF], col[:, C_B1:C_B1 + NF],
                                  ALU.add).then_inc(late_done, 1)
                dve.wait_ge(rows_in, 16)
                dve.tensor_tensor(bog[:, :], row[:, 0, :], row[:, 1, :], ALU.add).then_inc(late_done, 1)
                dve.wait_ge(late_done, 2)
                dve.wait_ge(late_mm, 2)
                dve.tensor_tensor(bias_t2[:, :], lin[1][:, 0:D], bog[:, :], ALU.add).then_inc(late_done, 1)

            def low_part(dst, bank_, hi, hi_sem, count, split):
                dve.wait_ge(hi_sem, count)
                dve.tensor_tensor(dst, halves(bank_), hi, ALU.subtract).then_inc(split, 1)

            def step(j, p, has_a, has_b, has_c):
                i = 2 * j + p
                q = 1 - p
                c = i - 2
                for h in range(HEADS + 1):
                    s = h - 1
                    if has_c and s in SLOT_OT:
                        u = SLOT_OT.index(s)
                        wide = ot_bank[u][:, :].rearrange("p (t h c) -> p t h c", t=NT, c=COLS)
                        heads = slice(u * HEADS // 2, (u + 1) * HEADS // 2)
                        dve.wait_ge(ot_ready, c * 2 + u + 1)
                        dve.reciprocal(recip[:, :, heads], wide[:, :, :, HD]).then_inc(recip_done, 1)
                        dve.wait_ge(recip_done, c * 2 + u + 1)
                        dve.tensor_tensor(o_norm[:, :, heads, :], wide[:, :, :, 0:HD],
                                          recip[:, :, heads].unsqueeze(3).to_broadcast([P, NT, HEADS // 2, HD]),
                                          ALU.mult).then_inc(o_done, 1)
                    if has_c and s == SLOT_ON:
                        low_part(oT[1][:, :, :], on_bank, oT[0][:, :, :], on_hi, c + 1, on_split)
                    if has_a and s == SLOT_XT:
                        low_part(xT[1][:, :, :], xt_bank, xT[0][:, :, :], xt_hi, i + 1, xt_split)
                    if has_c and s == SLOT_PROJ:
                        dve.wait_ge(proj_ready, c + 1)
                        dve.wait_ge(x_bias_done, c + 1)
                        dve.tensor_tensor(t2[:, :, :], halves(proj_bank), x_bias[:, :, :],
                                          ALU.add).then_inc(t2_done, 1)
                        dve.wait_ge(t2_done, c + 1)
                        moments(t2, stats2, mv2, var2, (st2_done, mv2_done, var2_done), c)
                    if has_c and s == SLOT_PROJ + 1:
                        normalize(t2, mv2, rstd2, tn, rstd2_done, tn_done, c)
                    for slot, kind, bank_, hi, split in ((SLOT_Q, 0, q_bank, q_hi, q_split),
                                                         (SLOT_K, 1, k_bank, k_hi, k_split)):
                        if has_a and s == slot:
                            dve.wait_ge(hi, (i + 1) * NK)
                            for m in range(NK):
                                bias = (bias_q[:, m:m + 1], bias_qkv[:, NK + m:NK + m + 1])[kind]
                                dve.scalar_tensor_tensor(qk_parts[:, kind, 1, m, :], halves(bank_)[:, m, :],
                                                         bias, qk_parts[:, kind, 0, m, :],
                                                         ALU.add, ALU.subtract).then_inc(split, 1)
                    if has_c and s == SLOT_L2T:
                        low_part(tT[1][:, :, :], l2t_bank, tT[0][:, :, :], l2t_hi, c + 1, l2t_split)
                    if has_c and s in SLOT_F1:
                        u = SLOT_F1.index(s)
                        dve.wait_ge(f1_hi, c * NF + 2 * u + 2)
                        if u >= 2:
                            dve.wait_ge(f1_split, c * UNITS + u - 1)
                        for half in range(2):
                            m = 2 * u + half
                            dve.tensor_scalar(relu32[:, u % 2, half, :], halves(f1_bank[u])[:, half, :],
                                              bias_h[:, m:m + 1], 0.0, ALU.add, ALU.max).then_inc(f1_relu, 1)
                    if h < HEADS and has_b:
                        b = i - 1
                        ring = h % SM_RING
                        dve.wait_ge(scores_ready, b * HEADS + h + 1)
                        if h == 0:
                            dve.wait_ge(mask_ready, b + 1)
                        if not isinstance(b, int) or b * HEADS + h >= SM_RING:
                            dve.wait_ge(turned, b * HEADS + h + 1 - SM_RING)
                        dve.sem_inc(dve_passed, 1)
                        for t in range(NT):
                            dve.tensor_tensor_reduce(masked[:, ring, t, :], halves(score_bank[h % 2])[:, t, :],
                                                     mask_bias[q][:, t, :], 1.0, LOWEST, ALU.add, ALU.max,
                                                     top[:, ring, t:t + 1]).then_inc(max_done, 1)
                    if has_a and h == SLOT_LN1 and not (isinstance(i, int) and i == 0):
                        dve.wait_ge(x_loaded[p], nth_of_parity(i, p, 16))
                        moments(x_in[p], stats1, mv1, var1, (st1_done, mv1_done, var1_done), i)
                    if has_a and h == SLOT_LN1 + 1 and not (isinstance(i, int) and i == 0):
                        dve.wait_ge(xt_ready, i)
                        normalize(x_in[p], mv1, rstd1, xn, rstd1_done, xn_done, i)
                if has_c:
                    dve.wait_ge(f2_ready, c + 1)
                    dve.wait_ge(t2_b2_done, c + 1)
                    dve.wait_ge(y_free, (c + 1) * 16)
                    dve.tensor_tensor(y[:, :, :], halves(f2_bank), t2_b2[:, :, :], ALU.add).then_inc(y_done, 1)
                if isinstance(i, int) and i == 0:
                    late_setup()

            run_steps(dve, step)

        @block.gpsimd
        def _(pool):
            pool.memset(minus_half[:, :], -0.5).then_inc(half_set, 1)

            def inverse_root(rstd, var, var_done, rstd_done, b):
                pool.wait_ge(var_done, b + 1)
                pool.tensor_tensor(rstd[:, :], var[:, :], minus_half[:, :], ALU.pow).then_inc(rstd_done, 1)

            pool.wait_ge(half_set, 1)
            inverse_root(rstd1, var1, var1_done, rstd1_done, 0)
            for p in range(2):
                pool.memset(v_cols[p][:, :, :, HD:HD + 1], 1.0).then_inc(zeroed, 1)
                pool.memset(v_cols[p][:, :, :, HD + 1:COLS], 0.0).then_inc(zeroed, 1)
            pool.wait_ge(zeroed, 4)
            for p in range(2):
                for t in (q_stack[p], k_stack[p]):
                    pool.memset(t[len(Q_PARTS) * HD:STACK, :, :], 0.0).then_inc(zeroed, 1)
            pool.wait_ge(zeroed, 8)

            def late_weights():
                for n, (lo, full, hi) in enumerate(
                        [(w_lo[:, w, :, :], w_raw[:, w, :, :], w_hi[:, w, :, :]) for w in (WO, WG)]
                        + [(w1_lo[:, :, :], w1_scaled[:, :, :], w1_hi[:, :, :]),
                           (w2_lo[:, :, :], w2_raw[:, :, :], w2_hi[:, :, :])]):
                    pool.wait_ge(wx_hi_done, n + 1)
                    pool.tensor_tensor(lo, full, hi, ALU.subtract).then_inc(wx_lo_done, 1)

            def rows_over_tiles(r):
                return r.unsqueeze(1).to_broadcast([P, NT, D])

            def step(j, p, has_a, has_b, has_c):
                i = 2 * j + p
                c = i - 2
                for h in range(HEADS):
                    sb_, sh, present = behind(i, h, 1, has_b, has_c)
                    if present:
                        ring = sh % SM_RING
                        pool.wait_ge(max_done, (sb_ * HEADS + sh + 1) * NT)
                        pool.tensor_tensor(masked[:, ring, :, :], masked[:, ring, :, :],
                                           top[:, ring, :].unsqueeze(2).to_broadcast([P, NT, S]),
                                           ALU.subtract).then_inc(sub_done, 1)
                    if has_c and h == SLOT_CTX:
                        pool.wait_ge(ctx_hi, c + 1)
                        pool.tensor_tensor(cT[1][:, :, :], ctx_in[p][:, :, :], cT[0][:, :, :],
                                           ALU.subtract).then_inc(ctx_split, 1)
                    if has_c and h == SLOT_CTX + 3:
                        pool.wait_ge(res_loaded[p], nth_of_parity(c, p, 16))
                        pool.wait_ge(late_done, 3)
                        pool.tensor_tensor(x_bias[:, :, :], x_res[p][:, :, :], rows_over_tiles(bias_t2[:, :]),
                                           ALU.add).then_inc(x_bias_done, 1)
                    if has_a and h == SLOT_LN1 and not (isinstance(i, int) and i == 0):
                        inverse_root(rstd1, var1, var1_done, rstd1_done, i)
                    if has_c and h == SLOT_PROJ + 1:
                        inverse_root(rstd2, var2, var2_done, rstd2_done, c)
                    if has_a and h == SLOT_PROJ:
                        pool.wait_ge(mask_loaded[p], nth_of_parity(i, p, 16))
                        if not isinstance(i, int) or i >= 2:
                            pool.wait_ge(max_done, (i - 1) * HEADS * NT)
                        pool.sem_inc(pool_passed, 1)
                        pool.tensor_scalar(mask_bias[p][:, :, :], mask_in[p][:, :, :], 1.0, MASKED,
                                           ALU.subtract, ALU.mult).then_inc(mask_ready, 1)
                    if has_c and h == SLOT_PROJ + 2:
                        pool.wait_ge(t2_done, c + 1)
                        pool.tensor_tensor(t2_b2[:, :, :], t2[:, :, :], rows_over_tiles(row[:, 2, :]),
                                           ALU.add).then_inc(t2_b2_done, 1)
                    if has_c and h - 1 in SLOT_F1:
                        u = SLOT_F1.index(h - 1)
                        pool.wait_ge(f1_relu, c * NF + 2 * u + 2)
                        pool.tensor_tensor(hid[1][:, 2 * u:2 * u + 2, :], relu32[:, u % 2, :, :],
                                           hid[0][:, 2 * u:2 * u + 2, :], ALU.subtract).then_inc(f1_split, 1)
                if isinstance(i, int) and i == 0:
                    late_weights()

            run_steps(pool, step)


def kernel(**inputs):
    import numpy as np
    import concourse.bacc as bacc
    from concourse.bass_utils import run_bass_kernel_spmd

    a = {k.replace("L0_xattn_", ""): np.asarray(v) for k, v in inputs.items()}

    def columns(v):
        return v.reshape(-1, P).T

    arrays = {
        "x": a["x"],
        "ctxT": a["ctx_1024"].transpose(0, 2, 1),
        "mask": a["mask_BxSxS2_fk0"],
        "WqT": a["Wq"].T, "WkT": a["Wk"].T, "WvT": a["Wv"].T, "WoT": a["Wo"].T, "WgT": a["Wg"].T,
        "W1T": a["W1"].T, "W2T": a["W2"].T,
        "cols": np.concatenate([columns(a[n]) for n in ("g1", "be1", "bq", "bk", "bv", "g2", "be2", "b1")], axis=1),
        "rows": np.stack([a["bo"], a["bg"], a["b2"]]),
        "eye": np.eye(P, dtype=np.float32),
    }
    arrays = {f"in_{k}": np.ascontiguousarray(v) for k, v in arrays.items()}
    nc = bacc.Bacc("TRN2", target_bir_lowering=False, num_devices=1)
    args = [nc.dram_tensor(k, v.shape, mybir.dt.from_np(v.dtype), kind="ExternalInput").ap()
            for k, v in arrays.items()]
    args.append(nc.dram_tensor("out", (BATCHES, S, D), F32, kind="ExternalOutput").ap())
    build(nc, *args)
    r = run_bass_kernel_spmd(nc, [arrays], core_ids=[0])
    return r.results[0]["out"]
```

```python
from contextlib import ExitStack

import concourse.bass as bass
from concourse import mybir

F32 = mybir.dt.float32
F16 = mybir.dt.float16
BF16 = mybir.dt.bfloat16
ALU = mybir.AluOpType
ACT = mybir.ActivationFunctionType

P = 128
BATCHES, S, D = 8, 256, 256
HEADS = 16
HD = D // HEADS
FF = 1024
NT = S // P
NK = D // P
NF = FF // P
UNITS = NF // 2
EPS = 1e-5
MASKED = 1e9
LOWEST = -3.4e38
SCALE = HD ** -0.5

GROUP = 4
GROUPS = HEADS // GROUP
COLS = P // GROUP
T_LAG = 2
SM_RING = 4
PT_RING = 8
PARTS = 2
STACK = 80

Q_PARTS = (0, 0, 1, 1)
K_PARTS = (0, 1, 0, 1)

C_G1, C_BE1, C_B, C_G2, C_BE2, C_B1 = 0, 2, 4, 10, 12, 14
N_COLS = 22
WQ, WK, WV, WO, WG = range(5)

SLOT_V = 0
SLOT_OT = (1, 3)
SLOT_PROJ_CTX = (1, 2)
SLOT_LN1, SLOT_XT = 1, 3
SLOT_Q, SLOT_K = 5, 8
SLOT_X_BIAS = 4
SLOT_ON, SLOT_PROJ_O = 4, 6
SLOT_MASK = 11
SLOT_L2T = 9
SLOT_F1 = (10, 11, 12, 13)
SLOT_F2 = {13: (0,), 14: (1,), 15: (2, 3)}
SLOT_T2_B2 = 12
SLOT_CTX = 13


def build(nc, x, ctxT, mask, wqT, wkT, wvT, woT, wgT, w1T, w2T, cols, rows, eye, out):
    x_t, mask_t, ctx_t, out_t = (v.rearrange("(j e) (t p) d -> j e p t d", e=2, p=P) for v in (x, mask, ctxT, out))
    scratch = nc.dram_tensor("qk_scratch", [2, 2, PARTS, D, S], F16, kind="Internal").ap()

    with ExitStack() as stack:
        def sb(name, shape, dt=F32):
            return stack.enter_context(nc.sbuf_tensor(name, shape, dt))

        def bank(name):
            return stack.enter_context(nc.psum_tensor(name, [P, 512], F32))

        def sem(name):
            return stack.enter_context(nc.semaphore(name))

        w_raw = sb("w_raw", [P, 5, NK, D])
        w1_raw = sb("w1_raw", [P, NK, FF])
        w2_raw = sb("w2_raw", [P, NF, D])
        w_scaled = sb("w_scaled", [P, 3, NK, D])
        w1_scaled = sb("w1_scaled", [P, NK, FF])
        w_hi = sb("w_hi", [P, 5, NK, D], F16)
        w_lo = sb("w_lo", [P, 5, NK, D], BF16)
        w1_hi = sb("w1_hi", [P, NK, FF], F16)
        w1_lo = sb("w1_lo", [P, NK, FF], BF16)
        w2_hi = sb("w2_hi", [P, NF, D], F16)
        w2_lo = sb("w2_lo", [P, NF, D], BF16)
        col = sb("col", [P, N_COLS])
        row = sb("row", [P, 3, D])
        ident = sb("ident", [P, P])
        bias_qkv = sb("bias_qkv", [P, 6])
        bias_q = sb("bias_q", [P, 2])
        bias_h = sb("bias_h", [P, NF])
        bv_wide = sb("bv_wide", [P, NK, P])
        minus_half = sb("minus_half", [P, NT])
        bog = sb("bog", [P, D])
        bias_t2 = sb("bias_t2", [P, D])

        x_in = [sb(f"x_in{p}", [P, NT, D]) for p in range(2)]
        stats1 = sb("stats1", [P, NT, 6])
        mv1 = sb("mv1", [P, NT, 2])
        var1, rstd1 = sb("var1", [P, NT]), sb("rstd1", [P, NT])
        xn = sb("xn", [P, NT, D])
        xT = [sb(f"xT{q}", [P, NK, S], F16) for q in range(PARTS)]
        qk_parts = sb("qk_parts", [P, 2, PARTS, NK, S], F16)
        q_stack = [sb(f"q_stack{p}", [STACK, HEADS, S], F16) for p in range(2)]
        k_stack = [sb(f"k_stack{p}", [STACK, HEADS, S], F16) for p in range(2)]
        v_cols = [sb(f"v_cols{p}", [P, NT, HEADS, COLS]) for p in range(2)]
        mask_in = [sb(f"mask_in{p}", [P, NT, S]) for p in range(2)]
        mask_bias = [sb(f"mask_bias{p}", [P, NT, S]) for p in range(2)]

        masked = sb("masked", [P, SM_RING, NT, S])
        top = sb("top", [P, SM_RING, NT])
        probsT = sb("probsT", [P, PT_RING, NT, S])

        oT_wide = sb("oT_wide", [P, GROUPS, S])
        recip = sb("recip", [P, NT, HEADS])
        o_norm = sb("o_norm", [P, NT, HEADS, HD])
        oT = [sb(f"oT{q}", [P, NK, S], F16) for q in range(PARTS)]
        ctx_in = [sb(f"ctx_in{p}", [P, NK, S]) for p in range(2)]
        cT = [sb(f"cT{q}", [P, NK, S], F16) for q in range(PARTS)]
        x_res = [sb(f"x_res{p}", [P, NT, D]) for p in range(2)]
        x_bias = sb("x_bias", [P, NT, D])
        t2 = sb("t2", [P, NT, D])
        t2_b2 = sb("t2_b2", [P, NT, D])
        stats2 = sb("stats2", [P, NT, 6])
        mv2 = sb("mv2", [P, NT, 2])
        var2, rstd2 = sb("var2", [P, NT]), sb("rstd2", [P, NT])
        tn = sb("tn", [P, NT, D])
        tT = [sb(f"tT{q}", [P, NK, S], F16) for q in range(PARTS)]
        relu32 = sb("relu32", [P, 2, 2, S])
        hid = [sb(f"hid{q}", [P, NF, S], F16) for q in range(PARTS)]
        y = sb("y", [P, NT, D])

        score_bank = [bank(f"score_bank{n}") for n in range(2)]
        turn_bank = [bank(f"turn_bank{n}") for n in range(2)]
        av_bank = bank("av_bank")
        lin = [bank(f"lin{n}") for n in range(3)]

        def halves(t):
            return t[:, :].rearrange("p (h c) -> p h c", h=2)

        v_bank, ot_bank, proj_bank, xt_bank = lin[2], [lin[0], lin[2]], lin[1], lin[0]
        q_bank, on_bank, k_bank, l2t_bank = lin[0], lin[2], lin[0], lin[2]
        f1_bank, f2_bank = [lin[1], lin[0], lin[2], lin[1]], lin[0]

        cols_in, eye_in, rows_in = sem("cols_in"), sem("eye_in"), sem("rows_in")
        qkv_in, og_in, w1_in, w2_in = sem("qkv_in"), sem("og_in"), sem("w1_in"), sem("w2_in")
        x_loaded = [sem(f"x_loaded{p}") for p in range(2)]
        mask_loaded = [sem(f"mask_loaded{p}") for p in range(2)]
        ctx_loaded = [sem(f"ctx_loaded{p}") for p in range(2)]
        res_loaded = [sem(f"res_loaded{p}") for p in range(2)]
        scratch_written = sem("scratch_written")
        stacked = [sem(f"stacked{p}") for p in range(2)]
        y_free = sem("y_free")
        dve_passed, sp_passed = sem("dve_passed"), sem("sp_passed")
        w_scaled_done, w_hi_done, w_lo_done = sem("w_scaled_done"), sem("w_hi_done"), sem("w_lo_done")
        wx_hi_done, wx_lo_done, w1_scaled_done = sem("wx_hi_done"), sem("wx_lo_done"), sem("w1_scaled_done")
        bias_mm, bias_done, late_mm, late_done = sem("bias_mm"), sem("bias_done"), sem("late_mm"), sem("late_done")
        zeroed, half_set = sem("zeroed"), sem("half_set")
        st1_done, mv1_done, var1_done = sem("st1_done"), sem("mv1_done"), sem("var1_done")
        rstd1_done, xn_done = sem("rstd1_done"), sem("xn_done")
        xt_ready, xt_hi, xt_split = sem("xt_ready"), sem("xt_hi"), sem("xt_split")
        q_ready, q_hi, q_split = sem("q_ready"), sem("q_hi"), sem("q_split")
        k_ready, k_hi, k_split = sem("k_ready"), sem("k_hi"), sem("k_split")
        v_ready, v_copied = sem("v_ready"), sem("v_copied")
        mask_ready = sem("mask_ready")
        scores_ready, max_done, sub_done = sem("scores_ready"), sem("max_done"), sem("sub_done")
        turned, exp_done, av_ready, av_copied = sem("turned"), sem("exp_done"), sem("av_ready"), sem("av_copied")
        ot_ready, recip_done, o_done = sem("ot_ready"), sem("recip_done"), sem("o_done")
        on_ready, on_hi, on_split = sem("on_ready"), sem("on_hi"), sem("on_split")
        ctx_hi, ctx_split, x_bias_done = sem("ctx_hi"), sem("ctx_split"), sem("x_bias_done")
        proj_ready, t2_done, t2_b2_done = sem("proj_ready"), sem("t2_done"), sem("t2_b2_done")
        st2_done, mv2_done, var2_done = sem("st2_done"), sem("mv2_done"), sem("var2_done")
        rstd2_done, tn_done = sem("rstd2_done"), sem("tn_done")
        l2t_ready, l2t_hi, l2t_split = sem("l2t_ready"), sem("l2t_hi"), sem("l2t_split")
        f1_ready, f1_hi, f1_relu, f1_split = sem("f1_ready"), sem("f1_hi"), sem("f1_relu"), sem("f1_split")
        f2_ready, y_done = sem("f2_ready"), sem("y_done")

        def nth_of_parity(b, p, each):
            return (b - p) * (each // 2) + each

        def run_steps(eng, step):
            step(0, 0, True, False, False)
            step(0, 1, True, True, False)
            with eng.Fori(1, BATCHES // 2) as j:
                step(j, 0, True, True, True)
                step(j, 1, True, True, True)
            step(BATCHES // 2, 0, False, True, True)
            step(BATCHES // 2, 1, False, False, True)

        def batch(tensor, j, p, back):
            return tensor[j + (p - back) // 2, (p - back) % 2]

        def behind(i, h, lag, has_b, has_c):
            return (i - 1, h - lag, has_b) if h >= lag else (i - 2, HEADS + h - lag, has_c)

        block = stack.enter_context(nc.Block())

        @block.sync
        def _(sp):
            sp.dma_start(col[:, :], cols).then_inc(cols_in, 16)
            sp.dma_start(x_in[0][:, :, :], x_t[0, 0]).then_inc(x_loaded[0], 16)
            for n, w in ((WQ, wqT), (WK, wkT), (WV, wvT)):
                sp.dma_start(w_raw[:, n, :, :], w.rearrange("(k p) n -> p k n", p=P)).then_inc(qkv_in, 16)
            sp.dma_start(ident[:, :], eye).then_inc(eye_in, 16)
            for n, w in ((WO, woT), (WG, wgT)):
                sp.dma_start(w_raw[:, n, :, :], w.rearrange("(k p) n -> p k n", p=P)).then_inc(og_in, 16)
            sp.dma_start(row[:, :, :], rows.partition_broadcast(P)).then_inc(rows_in, 16)

            def step(j, p, has_a, has_b, has_c):
                i = 2 * j + p
                q = 1 - p
                if has_a:
                    if not isinstance(i, int) or i >= 2:
                        sp.wait_ge(xn_done, (i - 1) * NT)
                        sp.sem_inc(sp_passed, 1)
                    if not isinstance(i, int) or i >= 1:
                        sp.dma_start(x_in[p][:, :, :], batch(x_t, j, p, 0)).then_inc(x_loaded[p], 16)
                    if not isinstance(i, int) or i >= 2:
                        sp.wait_ge(mask_ready, i - 1)
                        sp.sem_inc(sp_passed, 1)
                    sp.dma_start(mask_in[p][:, :, :], batch(mask_t, j, p, 0)).then_inc(mask_loaded[p], 16)
                if has_b:
                    sp.dma_start(ctx_in[q][:, :, :], batch(ctx_t, j, p, 1)).then_inc(ctx_loaded[q], 16)
                    sp.dma_start(x_res[q][:, :, :], batch(x_t, j, p, 1)).then_inc(res_loaded[q], 16)
                if has_a:
                    if not isinstance(i, int) or i >= 2:
                        sp.wait_ge(stacked[p], nth_of_parity(i - 2, p, 16 * 8))
                        sp.sem_inc(sp_passed, 1)
                        sp.wait_ge(scores_ready, (i - 1) * HEADS)
                        sp.sem_inc(sp_passed, 1)
                    sp.wait_ge(q_split, (i + 1) * NK)
                    sp.sem_inc(sp_passed, 1)
                    sp.dma_start(scratch[p, 0].rearrange("t (k p) s -> p t k s", p=P),
                                 qk_parts[:, 0, :, :, :]).then_inc(scratch_written, 16)
                    sp.wait_ge(k_split, (i + 1) * NK)
                    sp.sem_inc(sp_passed, 1)
                    sp.dma_start(scratch[p, 1].rearrange("t (k p) s -> p t k s", p=P),
                                 qk_parts[:, 1, :, :, :]).then_inc(scratch_written, 16)
                    sp.wait_ge(scratch_written, (i + 1) * 32)
                    sp.sem_inc(sp_passed, 1)
                    for kind, dst, parts in ((0, q_stack[p], Q_PARTS), (1, k_stack[p], K_PARTS)):
                        for n, part in enumerate(parts):
                            sp.dma_start(dst[n * HD:(n + 1) * HD, :, :],
                                         scratch[p, kind, part].rearrange("(h r) s -> r h s", r=HD)
                                         ).then_inc(stacked[p], 16)

            run_steps(sp, step)

        @block.tensor
        def _(pe):
            def turn(dst, src):
                for k in range(2):
                    for t in range(2):
                        last = pe.transpose(dst[:, k, t * P:(t + 1) * P], src[:, t, k * P:(k + 1) * P],
                                            ident[:, :])
                return last

            def product(dst, left, right, start, stop, open_group=False):
                pairs = ((0, 0), (1, 0), (0, 1))
                for n, (a, b) in enumerate(pairs):
                    last = pe.matmul(dst, left[a], right[b], start=start and n == 0,
                                     stop=stop and n == len(pairs) - 1, skip_group_check=open_group)
                return last

            def bias_qkv_products():
                pe.wait_ge(cols_in, 16)
                pe.wait_ge(qkv_in, 48)
                for w in range(3):
                    for m in range(NK):
                        for k in range(NK):
                            last = pe.matmul(lin[1][:, 2 * w + m:2 * w + m + 1],
                                             w_raw[:, w, k, m * P:(m + 1) * P],
                                             col[:, C_BE1 + k:C_BE1 + k + 1], start=k == 0, stop=k == NK - 1)
                last.then_inc(bias_mm, 1)

            def late_bias_products():
                pe.wait_ge(w1_in, 16)
                pe.wait_ge(k_split, NK)
                for m in range(NF):
                    for k in range(NK):
                        last = pe.matmul(lin[0][:, m:m + 1], w1_raw[:, k, m * P:(m + 1) * P],
                                         col[:, C_BE2 + k:C_BE2 + k + 1], start=k == 0, stop=k == NK - 1)
                last.then_inc(late_mm, 1)
                pe.wait_ge(og_in, 32)
                pe.wait_ge(bias_done, 3)
                for k in range(NK):
                    last = pe.matmul(lin[1][:, 0:D], bv_wide[:, k, :], w_raw[:, WO, k, :],
                                     start=k == 0, stop=k == NK - 1)
                last.then_inc(late_mm, 1)

            def scores(b, h, p):
                if h == 0:
                    pe.wait_ge(stacked[p], nth_of_parity(b, p, 16 * 8))
                if not isinstance(b, int) or b * HEADS + h >= 2:
                    pe.wait_ge(max_done, b * HEADS * NT + (h - 1) * NT)
                for t in range(NT):
                    last = pe.matmul(halves(score_bank[h % 2])[:, t, :], q_stack[p][:, h, t * P:(t + 1) * P],
                                     k_stack[p][:, h, :], start=True, stop=True)
                last.then_inc(scores_ready, 1)

            def turn_scores(b, h):
                pe.wait_ge(sub_done, b * HEADS + h + 1)
                if not isinstance(b, int) or b * HEADS + h >= 2:
                    pe.wait_ge(exp_done, b * HEADS + h - 1)
                turn(halves(turn_bank[h % 2]), masked[:, h % SM_RING, :, :]).then_inc(turned, 1)

            def apply_v(b, g, p):
                if g == 0:
                    pe.wait_ge(v_copied, b + 1)
                pe.wait_ge(exp_done, b * HEADS + (g + 1) * GROUP)
                if not isinstance(b, int) or b * GROUPS + g >= 1:
                    pe.wait_ge(av_copied, b * GROUPS + g)
                for t in range(NT):
                    for j in range(GROUP):
                        h = g * GROUP + j
                        last = pe.matmul(av_bank[j * COLS:(j + 1) * COLS, 0:S], v_cols[p][:, t, h, :],
                                         probsT[:, h % PT_RING, t, :], start=t == 0, stop=t == NT - 1,
                                         skip_group_check=True)
                last.then_inc(av_ready, 1)

            def project(bank_, w):
                for m in range(NK):
                    for k in range(NK):
                        last = product(halves(bank_)[:, m, :],
                                       [t[:, w, k, m * P:(m + 1) * P] for t in (w_hi, w_lo)],
                                       [xT[0][:, k, :], xT[1][:, k, :]], k == 0, k == NK - 1)
                return last

            def step(j, p, has_a, has_b, has_c):
                i = 2 * j + p
                q = 1 - p
                c = i - 2
                if isinstance(i, int) and i == 1:
                    pe.wait_ge(late_done, 3)
                    pe.wait_ge(zeroed, 8)
                for h in range(HEADS):
                    if has_b:
                        scores(i - 1, h, q)
                    tb, th, present = behind(i, h, T_LAG, has_b, has_c)
                    if present:
                        turn_scores(tb, th)
                    if h % GROUP == T_LAG % GROUP:
                        tb, th, present = behind(i, h, T_LAG + GROUP, has_b, has_c)
                        if present:
                            apply_v(tb, th // GROUP, q if h >= T_LAG + GROUP else p)
                    if has_b and h == SLOT_V:
                        if not isinstance(i, int) or i >= 2:
                            pe.wait_ge(v_copied, i - 1)
                        for t in range(NT):
                            for k in range(NK):
                                last = product(halves(v_bank)[:, t, :],
                                               [z[:, k, t * P:(t + 1) * P] for z in xT],
                                               [w_hi[:, WV, k, :], w_lo[:, WV, k, :]], k == 0, k == NK - 1)
                        last.then_inc(v_ready, 1)
                    if has_c and h in SLOT_OT:
                        u = SLOT_OT.index(h)
                        pe.wait_ge(av_copied, c * GROUPS + 2 * u + 2)
                        if u == 0 and has_b:
                            pe.wait_ge(max_done, (i - 1) * HEADS * NT + NT)
                        elif u == 0:
                            pe.wait_ge(y_done, c)
                        elif has_b:
                            pe.wait_ge(v_copied, i)
                        dst = ot_bank[u][:, :].rearrange("p (t g c) -> p t g c", t=NT, g=2)
                        for g in range(2):
                            for t in range(NT):
                                last = pe.transpose(dst[:, t, g, :],
                                                    oT_wide[:, 2 * u + g, t * P:(t + 1) * P], ident[:, :])
                        last.then_inc(ot_ready, 1)
                    if has_c and h in SLOT_PROJ_CTX:
                        t = SLOT_PROJ_CTX.index(h)
                        if t == 0:
                            pe.wait_ge(wx_lo_done, 2)
                            pe.wait_ge(ctx_split, c + 1)
                        for k in range(NK):
                            product(halves(proj_bank)[:, t, :], [z[:, k, t * P:(t + 1) * P] for z in cT],
                                    [w_hi[:, WG, k, :], w_lo[:, WG, k, :]], t == 0 and k == 0, False,
                                    open_group=True)
                    if has_a and h == SLOT_XT:
                        if isinstance(i, int) and i == 0:
                            pe.wait_ge(eye_in, 16)
                        pe.wait_ge(xn_done, (i + 1) * NT)
                        if has_c:
                            pe.wait_ge(o_done, c * 2 + 1)
                        elif i >= 1:
                            pe.wait_ge(k_split, i * NK)
                        turn(halves(xt_bank), xn[:, :, :]).then_inc(xt_ready, 1)
                    if has_c and h == SLOT_ON:
                        pe.wait_ge(o_done, (c + 1) * 2)
                        turn(halves(on_bank), o_norm[:, :, :, :].rearrange("p t h d -> p t (h d)")
                             ).then_inc(on_ready, 1)
                    if has_a and h == SLOT_Q:
                        if isinstance(i, int) and i == 0:
                            pe.wait_ge(w_lo_done, 3)
                        pe.wait_ge(xt_split, i + 1)
                        project(q_bank, WQ).then_inc(q_ready, 1)
                    if has_c and h == SLOT_PROJ_O:
                        pe.wait_ge(on_split, c + 1)
                        for t in range(NT):
                            for k in range(NK):
                                last = product(halves(proj_bank)[:, t, :], [z[:, k, t * P:(t + 1) * P] for z in oT],
                                               [w_hi[:, WO, k, :], w_lo[:, WO, k, :]], False, k == NK - 1,
                                               open_group=True)
                        last.then_inc(proj_ready, 1)
                    if has_a and h == SLOT_K:
                        pe.wait_ge(q_split, (i + 1) * NK)
                        project(k_bank, WK).then_inc(k_ready, 1)
                    if has_c and h == SLOT_L2T:
                        pe.wait_ge(tn_done, (c + 1) * NT)
                        turn(halves(l2t_bank), tn[:, :, :]).then_inc(l2t_ready, 1)
                    if has_c and h in SLOT_F1:
                        u = SLOT_F1.index(h)
                        if u == 0:
                            pe.wait_ge(wx_lo_done, 4)
                            pe.wait_ge(l2t_split, c + 1)
                        if u == 1 and has_a:
                            pe.wait_ge(k_split, (i + 1) * NK)
                        if u == 3:
                            pe.wait_ge(f1_relu, c * NF + 2)
                        for half in range(2):
                            m = 2 * u + half
                            for k in range(NK):
                                last = product(halves(f1_bank[u])[:, half, :],
                                               [w[:, k, m * P:(m + 1) * P] for w in (w1_hi, w1_lo)],
                                               [tT[0][:, k, :], tT[1][:, k, :]], k == 0, k == NK - 1)
                        last.then_inc(f1_ready, 1)
                    if has_c and h in SLOT_F2:
                        for u in SLOT_F2[h]:
                            pe.wait_ge(f1_split, c * UNITS + u + 1)
                            if u == 0:
                                pe.wait_ge(f1_relu, c * NF + 4)
                            for t in range(NT):
                                for k in (2 * u, 2 * u + 1):
                                    last = product(halves(f2_bank)[:, t, :], [z[:, k, t * P:(t + 1) * P] for z in hid],
                                                   [w2_hi[:, k, :], w2_lo[:, k, :]],
                                                   k == 0 and t == 0, k == NF - 1, open_group=True)
                            if u == UNITS - 1:
                                last.then_inc(f2_ready, 1)
                if isinstance(i, int) and i == 0:
                    late_bias_products()

            bias_qkv_products()
            run_steps(pe, step)

        @block.scalar
        def _(act):
            act.sem_inc(y_free, 16)
            act.dma_start(w1_raw[:, :, :], w1T.rearrange("(k p) n -> p k n", p=P)).then_inc(w1_in, 16)
            act.dma_start(w2_raw[:, :, :], w2T.rearrange("(k p) n -> p k n", p=P)).then_inc(w2_in, 16)
            for w in range(3):
                act.wait_ge(w_scaled_done, (w + 1) * NK)
                act.copy(w_hi[:, w, :, :], w_scaled[:, w, :, :]).then_inc(w_hi_done, 1)

            def late_weights():
                act.wait_ge(og_in, 32)
                for w in (WO, WG):
                    act.copy(w_hi[:, w, :, :], w_raw[:, w, :, :]).then_inc(wx_hi_done, 1)
                act.wait_ge(w1_scaled_done, NK)
                act.copy(w1_hi[:, :, :], w1_scaled[:, :, :]).then_inc(wx_hi_done, 1)
                act.wait_ge(w2_in, 16)
                act.copy(w2_hi[:, :, :], w2_raw[:, :, :]).then_inc(wx_hi_done, 1)

            def step(j, p, has_a, has_b, has_c):
                i = 2 * j + p
                q = 1 - p
                c = i - 2
                for h in range(HEADS):
                    tb, th, present = behind(i, h, T_LAG, has_b, has_c)
                    if present:
                        act.wait_ge(turned, tb * HEADS + th + 1)
                        if not isinstance(tb, int) or tb * HEADS + th >= PT_RING:
                            act.wait_ge(av_ready, tb * GROUPS + th // GROUP - 1)
                        act.activation(probsT[:, th % PT_RING, :, :], halves(turn_bank[th % 2]),
                                       ACT.Exp).then_inc(exp_done, 1)
                    if h % GROUP == T_LAG % GROUP:
                        tb, th, present = behind(i, h, T_LAG + GROUP, has_b, has_c)
                        if present:
                            g = th // GROUP
                            act.wait_ge(av_ready, tb * GROUPS + g + 1)
                            act.copy(oT_wide[:, g, :], av_bank[:, 0:S]).then_inc(av_copied, 1)
                    if has_c and h == SLOT_ON:
                        act.wait_ge(on_ready, c + 1)
                        act.copy(oT[0][:, :, :], halves(on_bank)).then_inc(on_hi, 1)
                    if has_a and h == SLOT_XT:
                        act.wait_ge(xt_ready, i + 1)
                        act.copy(xT[0][:, :, :], halves(xt_bank)).then_inc(xt_hi, 1)
                    for slot, kind, ready, bank_, hi in ((SLOT_Q, 0, q_ready, q_bank, q_hi),
                                                         (SLOT_K, 1, k_ready, k_bank, k_hi)):
                        if has_a and h == slot:
                            act.wait_ge(ready, i + 1)
                            if isinstance(i, int) and i == 0:
                                act.wait_ge(bias_done, 2)
                            if not isinstance(i, int) or i >= 1:
                                act.wait_ge(scratch_written, i * 32)
                            for m in range(NK):
                                bias = (bias_q[:, m:m + 1], bias_qkv[:, NK + m:NK + m + 1])[kind]
                                act.activation(qk_parts[:, kind, 0, m, :], halves(bank_)[:, m, :],
                                               ACT.Identity, bias=bias).then_inc(hi, 1)
                    if has_c and h == SLOT_L2T:
                        act.wait_ge(l2t_ready, c + 1)
                        act.copy(tT[0][:, :, :], halves(l2t_bank)).then_inc(l2t_hi, 1)
                    if has_c and h in SLOT_F1:
                        u = SLOT_F1.index(h)
                        act.wait_ge(f1_ready, c * UNITS + u + 1)
                        if u >= 2:
                            act.wait_ge(f1_split, c * UNITS + u - 1)
                        for half in range(2):
                            m = 2 * u + half
                            act.activation(relu32[:, u % 2, half, :], halves(f1_bank[u])[:, half, :], ACT.Relu,
                                           bias=bias_h[:, m:m + 1]).then_inc(f1_relu, 1)
                        act.wait_ge(f1_relu, c * NF + 2 * u + 2)
                        act.copy(hid[0][:, 2 * u:2 * u + 2, :], relu32[:, u % 2, :, :]).then_inc(f1_hi, 1)
                    if has_b and h == SLOT_CTX:
                        act.wait_ge(ctx_loaded[q], nth_of_parity(i - 1, q, 16))
                        act.copy(cT[0][:, :, :], ctx_in[q][:, :, :]).then_inc(ctx_hi, 1)
                    if has_b and h == SLOT_V:
                        act.wait_ge(v_ready, i)
                        if isinstance(i, int) and i == 1:
                            act.wait_ge(zeroed, 4)
                        act.copy(v_cols[q][:, :, :, 0:HD],
                                 halves(v_bank).rearrange("p t (h d) -> p t h d", d=HD)).then_inc(v_copied, 1)
                if isinstance(i, int) and i == 0:
                    late_weights()
                if isinstance(i, int) and i == 1:
                    act.wait_ge(late_done, 1)
                if has_c:
                    act.wait_ge(y_done, c + 1)
                    act.dma_start(batch(out_t, j, p, 2), y[:, :, :]).then_inc(y_free, 16)

            run_steps(act, step)
            act.wait_ge(y_free, (BATCHES + 1) * 16)

        @block.vector
        def _(dve):
            def moments(src, stats, mv, var, sems, b):
                st_done, mv_done, var_done = sems
                for t in range(NT):
                    dve.bn_stats(stats[:, t, :], src[:, t, :]).then_inc(st_done, 1)
                for t in range(NT):
                    dve.wait_ge(st_done, b * NT + t + 1)
                    dve.sem_inc(dve_passed, 1)
                    dve.bn_aggr(mv[:, t, :], stats[:, t, :]).then_inc(mv_done, 1)
                dve.wait_ge(mv_done, (b + 1) * NT)
                dve.tensor_scalar(var[:, :], mv[:, :, 1], EPS, None, ALU.add).then_inc(var_done, 1)

            def normalize(src, mv, rstd, dst, rstd_done, done, b):
                dve.wait_ge(rstd_done, b + 1)
                for t in range(NT):
                    dve.tensor_scalar(dst[:, t, :], src[:, t, :], mv[:, t, 0:1], rstd[:, t:t + 1],
                                      ALU.subtract, ALU.mult).then_inc(done, 1)

            dve.wait_ge(cols_in, 16)
            dve.wait_ge(qkv_in, 48)
            for w in range(3):
                for k in range(NK):
                    gain = col[:, C_G1 + k:C_G1 + k + 1]
                    dve.tensor_scalar(w_scaled[:, w, k, :], w_raw[:, w, k, :], gain,
                                      SCALE if w == WQ else 1.0, ALU.mult, ALU.mult).then_inc(w_scaled_done, 1)
            dve.wait_ge(x_loaded[0], 16)
            moments(x_in[0], stats1, mv1, var1, (st1_done, mv1_done, var1_done), 0)
            normalize(x_in[0], mv1, rstd1, xn, rstd1_done, xn_done, 0)
            for w in range(3):
                dve.wait_ge(w_hi_done, w + 1)
                dve.tensor_tensor(w_lo[:, w, :, :], w_scaled[:, w, :, :], w_hi[:, w, :, :],
                                  ALU.subtract).then_inc(w_lo_done, 1)
            dve.wait_ge(bias_mm, 1)
            dve.tensor_tensor(bias_qkv[:, :], lin[1][:, 0:6], col[:, C_B:C_B + 6], ALU.add).then_inc(bias_done, 1)
            dve.wait_ge(bias_done, 1)
            dve.tensor_scalar(bias_q[:, :], bias_qkv[:, 0:2], SCALE, None, ALU.mult).then_inc(bias_done, 1)
            dve.tensor_copy(bv_wide[:, :, :], bias_qkv[:, 4:6].unsqueeze(2).to_broadcast([P, NK, P])
                            ).then_inc(bias_done, 1)

            def late_setup():
                dve.wait_ge(w1_in, 16)
                for k in range(NK):
                    dve.tensor_scalar(w1_scaled[:, k, :], w1_raw[:, k, :], col[:, C_G2 + k:C_G2 + k + 1],
                                      None, ALU.mult).then_inc(w1_scaled_done, 1)
                dve.wait_ge(late_mm, 1)
                dve.tensor_tensor(bias_h[:, :], lin[0][:, 0:NF], col[:, C_B1:C_B1 + NF],
                                  ALU.add).then_inc(late_done, 1)
                dve.wait_ge(rows_in, 16)
                dve.tensor_tensor(bog[:, :], row[:, 0, :], row[:, 1, :], ALU.add).then_inc(late_done, 1)
                dve.wait_ge(late_done, 2)
                dve.wait_ge(late_mm, 2)
                dve.tensor_tensor(bias_t2[:, :], lin[1][:, 0:D], bog[:, :], ALU.add).then_inc(late_done, 1)

            def low_part(dst, bank_, hi, hi_sem, count, split):
                dve.wait_ge(hi_sem, count)
                dve.tensor_tensor(dst, halves(bank_), hi, ALU.subtract).then_inc(split, 1)

            def step(j, p, has_a, has_b, has_c):
                i = 2 * j + p
                q = 1 - p
                c = i - 2
                for h in range(HEADS + 1):
                    s = h - 1
                    if has_c and s in SLOT_OT:
                        u = SLOT_OT.index(s)
                        wide = ot_bank[u][:, :].rearrange("p (t h c) -> p t h c", t=NT, c=COLS)
                        heads = slice(u * HEADS // 2, (u + 1) * HEADS // 2)
                        dve.wait_ge(ot_ready, c * 2 + u + 1)
                        dve.reciprocal(recip[:, :, heads], wide[:, :, :, HD]).then_inc(recip_done, 1)
                        dve.wait_ge(recip_done, c * 2 + u + 1)
                        dve.tensor_tensor(o_norm[:, :, heads, :], wide[:, :, :, 0:HD],
                                          recip[:, :, heads].unsqueeze(3).to_broadcast([P, NT, HEADS // 2, HD]),
                                          ALU.mult).then_inc(o_done, 1)
                    if has_c and s == SLOT_ON:
                        low_part(oT[1][:, :, :], on_bank, oT[0][:, :, :], on_hi, c + 1, on_split)
                    if has_a and s == SLOT_XT:
                        low_part(xT[1][:, :, :], xt_bank, xT[0][:, :, :], xt_hi, i + 1, xt_split)
                    if has_c and s == SLOT_PROJ_O:
                        dve.wait_ge(proj_ready, c + 1)
                        dve.wait_ge(x_bias_done, c + 1)
                        dve.tensor_tensor(t2[:, :, :], halves(proj_bank), x_bias[:, :, :],
                                          ALU.add).then_inc(t2_done, 1)
                        dve.wait_ge(t2_done, c + 1)
                        moments(t2, stats2, mv2, var2, (st2_done, mv2_done, var2_done), c)
                    if has_c and s == SLOT_PROJ_O + 1:
                        normalize(t2, mv2, rstd2, tn, rstd2_done, tn_done, c)
                    for slot, kind, bank_, hi, split in ((SLOT_Q, 0, q_bank, q_hi, q_split),
                                                         (SLOT_K, 1, k_bank, k_hi, k_split)):
                        if has_a and s == slot:
                            dve.wait_ge(hi, (i + 1) * NK)
                            for m in range(NK):
                                bias = (bias_q[:, m:m + 1], bias_qkv[:, NK + m:NK + m + 1])[kind]
                                dve.scalar_tensor_tensor(qk_parts[:, kind, 1, m, :], halves(bank_)[:, m, :],
                                                         bias, qk_parts[:, kind, 0, m, :],
                                                         ALU.add, ALU.subtract).then_inc(split, 1)
                    if has_c and s == SLOT_L2T:
                        low_part(tT[1][:, :, :], l2t_bank, tT[0][:, :, :], l2t_hi, c + 1, l2t_split)
                    if has_c and s in SLOT_F1:
                        u = SLOT_F1.index(s)
                        dve.wait_ge(f1_hi, c * UNITS + u + 1)
                        dve.tensor_tensor(hid[1][:, 2 * u:2 * u + 2, :], relu32[:, u % 2, :, :],
                                          hid[0][:, 2 * u:2 * u + 2, :], ALU.subtract).then_inc(f1_split, 1)
                    if has_b and s == SLOT_CTX:
                        dve.wait_ge(ctx_hi, i)
                        dve.tensor_tensor(cT[1][:, :, :], ctx_in[q][:, :, :], cT[0][:, :, :],
                                          ALU.subtract).then_inc(ctx_split, 1)
                    if h < HEADS and has_b:
                        b = i - 1
                        ring = h % SM_RING
                        dve.wait_ge(scores_ready, b * HEADS + h + 1)
                        if h == 0:
                            dve.wait_ge(mask_ready, b + 1)
                        if not isinstance(b, int) or b * HEADS + h >= SM_RING:
                            dve.wait_ge(turned, b * HEADS + h + 1 - SM_RING)
                        dve.sem_inc(dve_passed, 1)
                        for t in range(NT):
                            dve.tensor_tensor_reduce(masked[:, ring, t, :], halves(score_bank[h % 2])[:, t, :],
                                                     mask_bias[q][:, t, :], 1.0, LOWEST, ALU.add, ALU.max,
                                                     top[:, ring, t:t + 1]).then_inc(max_done, 1)
                    if has_a and h == SLOT_LN1 and not (isinstance(i, int) and i == 0):
                        dve.wait_ge(x_loaded[p], nth_of_parity(i, p, 16))
                        moments(x_in[p], stats1, mv1, var1, (st1_done, mv1_done, var1_done), i)
                    if has_a and h == SLOT_LN1 + 1 and not (isinstance(i, int) and i == 0):
                        dve.wait_ge(xt_ready, i)
                        normalize(x_in[p], mv1, rstd1, xn, rstd1_done, xn_done, i)
                    if has_a and h == SLOT_MASK:
                        dve.wait_ge(mask_loaded[p], nth_of_parity(i, p, 16))
                        dve.tensor_scalar(mask_bias[p][:, :, :], mask_in[p][:, :, :], 1.0, MASKED,
                                          ALU.subtract, ALU.mult).then_inc(mask_ready, 1)
                if has_c:
                    dve.wait_ge(f2_ready, c + 1)
                    dve.wait_ge(t2_b2_done, c + 1)
                    dve.wait_ge(y_free, (c + 1) * 16)
                    dve.tensor_tensor(y[:, :, :], halves(f2_bank), t2_b2[:, :, :], ALU.add).then_inc(y_done, 1)
                if isinstance(i, int) and i == 0:
                    late_setup()

            run_steps(dve, step)

        @block.gpsimd
        def _(pool):
            pool.memset(minus_half[:, :], -0.5).then_inc(half_set, 1)

            def inverse_root(rstd, var, var_done, rstd_done, b):
                pool.wait_ge(var_done, b + 1)
                pool.tensor_tensor(rstd[:, :], var[:, :], minus_half[:, :], ALU.pow).then_inc(rstd_done, 1)

            pool.wait_ge(half_set, 1)
            inverse_root(rstd1, var1, var1_done, rstd1_done, 0)
            for p in range(2):
                pool.memset(v_cols[p][:, :, :, HD:HD + 1], 1.0).then_inc(zeroed, 1)
                pool.memset(v_cols[p][:, :, :, HD + 1:COLS], 0.0).then_inc(zeroed, 1)
            pool.wait_ge(zeroed, 4)
            for p in range(2):
                for t in (q_stack[p], k_stack[p]):
                    pool.memset(t[len(Q_PARTS) * HD:STACK, :, :], 0.0).then_inc(zeroed, 1)
            pool.wait_ge(zeroed, 8)

            def late_weights():
                for n, (lo, full, hi) in enumerate(
                        [(w_lo[:, w, :, :], w_raw[:, w, :, :], w_hi[:, w, :, :]) for w in (WO, WG)]
                        + [(w1_lo[:, :, :], w1_scaled[:, :, :], w1_hi[:, :, :]),
                           (w2_lo[:, :, :], w2_raw[:, :, :], w2_hi[:, :, :])]):
                    pool.wait_ge(wx_hi_done, n + 1)
                    pool.tensor_tensor(lo, full, hi, ALU.subtract).then_inc(wx_lo_done, 1)

            def rows_over_tiles(r):
                return r.unsqueeze(1).to_broadcast([P, NT, D])

            def step(j, p, has_a, has_b, has_c):
                i = 2 * j + p
                c = i - 2
                for h in range(HEADS):
                    sb_, sh, present = behind(i, h, 1, has_b, has_c)
                    if present:
                        ring = sh % SM_RING
                        pool.wait_ge(max_done, (sb_ * HEADS + sh + 1) * NT)
                        pool.tensor_tensor(masked[:, ring, :, :], masked[:, ring, :, :],
                                           top[:, ring, :].unsqueeze(2).to_broadcast([P, NT, S]),
                                           ALU.subtract).then_inc(sub_done, 1)
                    if has_c and h == SLOT_X_BIAS:
                        pool.wait_ge(res_loaded[p], nth_of_parity(c, p, 16))
                        pool.wait_ge(late_done, 3)
                        pool.tensor_tensor(x_bias[:, :, :], x_res[p][:, :, :], rows_over_tiles(bias_t2[:, :]),
                                           ALU.add).then_inc(x_bias_done, 1)
                    if has_a and h == SLOT_LN1 and not (isinstance(i, int) and i == 0):
                        inverse_root(rstd1, var1, var1_done, rstd1_done, i)
                    if has_c and h == SLOT_PROJ_O + 1:
                        inverse_root(rstd2, var2, var2_done, rstd2_done, c)
                    if has_c and h == SLOT_T2_B2:
                        pool.wait_ge(t2_done, c + 1)
                        pool.tensor_tensor(t2_b2[:, :, :], t2[:, :, :], rows_over_tiles(row[:, 2, :]),
                                           ALU.add).then_inc(t2_b2_done, 1)
                if isinstance(i, int) and i == 0:
                    late_weights()

            run_steps(pool, step)


def kernel(**inputs):
    import numpy as np
    import concourse.bacc as bacc
    from concourse.bass_utils import run_bass_kernel_spmd

    a = {k.replace("L0_xattn_", ""): np.asarray(v) for k, v in inputs.items()}

    def columns(v):
        return v.reshape(-1, P).T

    arrays = {
        "x": a["x"],
        "ctxT": a["ctx_1024"].transpose(0, 2, 1),
        "mask": a["mask_BxSxS2_fk0"],
        "WqT": a["Wq"].T, "WkT": a["Wk"].T, "WvT": a["Wv"].T, "WoT": a["Wo"].T, "WgT": a["Wg"].T,
        "W1T": a["W1"].T, "W2T": a["W2"].T,
        "cols": np.concatenate([columns(a[n]) for n in ("g1", "be1", "bq", "bk", "bv", "g2", "be2", "b1")], axis=1),
        "rows": np.stack([a["bo"], a["bg"], a["b2"]]),
        "eye": np.eye(P, dtype=np.float32),
    }
    arrays = {f"in_{k}": np.ascontiguousarray(v) for k, v in arrays.items()}
    nc = bacc.Bacc("TRN2", target_bir_lowering=False, num_devices=1)
    args = [nc.dram_tensor(k, v.shape, mybir.dt.from_np(v.dtype), kind="ExternalInput").ap()
            for k, v in arrays.items()]
    args.append(nc.dram_tensor("out", (BATCHES, S, D), F32, kind="ExternalOutput").ap())
    build(nc, *args)
    r = run_bass_kernel_spmd(nc, [arrays], core_ids=[0])
    return r.results[0]["out"]
```

```python
from contextlib import ExitStack

import concourse.bass as bass
from concourse import mybir

F32 = mybir.dt.float32
F16 = mybir.dt.float16
BF16 = mybir.dt.bfloat16
ALU = mybir.AluOpType
ACT = mybir.ActivationFunctionType

P = 128
BATCHES, S, D = 8, 256, 256
HEADS = 16
HD = D // HEADS
FF = 1024
NT = S // P
NK = D // P
NF = FF // P
UNITS = NF // 2
EPS = 1e-5
MASKED = 1e9
LOWEST = -3.4e38
SCALE = HD ** -0.5

GROUP = 4
GROUPS = HEADS // GROUP
COLS = P // GROUP
T_LAG = 2
SM_RING = 4
PT_RING = 8
PARTS = 2
STACK = 80

Q_PARTS = (0, 0, 1, 1)
K_PARTS = (0, 1, 0, 1)

C_BQ, C_BK, C_BV, C_B1 = 0, 2, 4, 6
N_COLS = 14
R_G1, R_BE1, R_G2, R_BE2, R_BO, R_BG, R_B2 = range(7)
N_ROWS = 7
FIRST_ROWS = 2
WQ, WK, WV, WO, WG, W1, W2 = range(7)
W1_PIECES = [slice(n, n + 1) for n in range(NK)]
W2_PIECES = [slice(n, n + 2) for n in range(0, NF, 2)]
PARTS_DONE = {WQ: 1, WK: 2, WV: 3, W1: 5, WO: 6, WG: 7, W2: 7 + len(W2_PIECES)}

SLOT_V = 8
SLOT_OT = (1, 3)
SLOT_PROJ_CTX = (1, 2)
SLOT_LN1, SLOT_XN, SLOT_XT = 1, 2, 3
SLOT_Q, SLOT_K = 5, 7
SLOT_Q_LOW, SLOT_K_LOW = 5, 9
SLOT_X_BIAS = 4
SLOT_ON, SLOT_PROJ_O = 4, 5
SLOT_T2, SLOT_TG, SLOT_LN2 = 6, 6, 8
SLOT_ROOT1, SLOT_ROOT2 = 1, 7
SLOT_T2_B2 = 12
SLOT_L2T = 9
SLOT_F1 = (10, 11, 12, 13)
SLOT_F2 = {12: (0,), 13: (1,), 14: (2,), 15: (3,)}
SLOT_MASK = 8
SLOT_CTX = 12
SLOT_OG_PARTS = (5, 7)
SLOT_W2_PARTS = (9, 10, 12, 13)
SLOT_LATE_K = 3
WARM_UP = 24
WARM_XT, WARM_Q, WARM_SCORES = 11, 9, 6
WARM_ON, WARM_PO, WARM_L2T, WARM_F1 = 4, 3, 26, 8


def build(nc, x, ctxT, mask, wqT, wkT, wvT, woT, wgT, w1T, w2T, cols, rows, eye, out):
    x_t, mask_t, ctx_t, out_t = (v.rearrange("(j e) (t p) d -> j e p t d", e=2, p=P) for v in (x, mask, ctxT, out))
    scratch = nc.dram_tensor("qk_scratch", [2, 2, PARTS, D, S], F16, kind="Internal").ap()

    with ExitStack() as stack:
        def sb(name, shape, dt=F32):
            return stack.enter_context(nc.sbuf_tensor(name, shape, dt))

        def bank(name):
            return stack.enter_context(nc.psum_tensor(name, [P, 512], F32))

        def sem(name):
            return stack.enter_context(nc.semaphore(name))

        w_raw = sb("w_raw", [P, 5, NK, D])
        w1_raw = sb("w1_raw", [P, NK, FF])
        w2_raw = sb("w2_raw", [P, NF, D])
        w_hi = sb("w_hi", [P, 5, NK, D], F16)
        w_lo = sb("w_lo", [P, 5, NK, D], BF16)
        w1_hi = sb("w1_hi", [P, NK, FF], F16)
        w1_lo = sb("w1_lo", [P, NK, FF], BF16)
        w2_hi = sb("w2_hi", [P, NF, D], F16)
        w2_lo = sb("w2_lo", [P, NF, D], BF16)
        col = sb("col", [P, N_COLS])
        row = sb("row", [P, N_ROWS, D])
        ident = sb("ident", [P, P])
        bias_q = sb("bias_q", [P, NK])
        bv_wide = sb("bv_wide", [P, NK, P])
        blank = sb("blank", [P, D], F16)
        minus_half = sb("minus_half", [P, NT])
        bog = sb("bog", [P, D])
        bias_t2 = sb("bias_t2", [P, D])

        x_in = [sb(f"x_in{p}", [P, NT, D]) for p in range(2)]
        stats1 = sb("stats1", [P, NT, 6])
        mv1 = sb("mv1", [P, NT, 2])
        var1, rstd1 = sb("var1", [P, NT]), sb("rstd1", [P, NT])
        xg = sb("xg", [P, NT, D])
        xn = sb("xn", [P, NT, D])
        xT = [sb(f"xT{q}", [P, NK, S], F16) for q in range(PARTS)]
        qk_parts = sb("qk_parts", [P, 2, PARTS, NK, S], F16)
        q_stack = [sb(f"q_stack{p}", [STACK, HEADS, S], F16) for p in range(2)]
        k_stack = [sb(f"k_stack{p}", [STACK, HEADS, S], F16) for p in range(2)]
        v_cols = [sb(f"v_cols{p}", [P, NT, HEADS, COLS]) for p in range(2)]
        mask_in = [sb(f"mask_in{p}", [P, NT, S]) for p in range(2)]
        mask_bias = [sb(f"mask_bias{p}", [P, NT, S]) for p in range(2)]

        masked = sb("masked", [P, SM_RING, NT, S])
        top = sb("top", [P, SM_RING, NT])
        probsT = sb("probsT", [P, PT_RING, NT, S])

        oT_wide = sb("oT_wide", [P, GROUPS, S])
        recip = sb("recip", [P, NT, HEADS])
        o_norm = sb("o_norm", [P, NT, HEADS, HD])
        oT = [sb(f"oT{q}", [P, NK, S], F16) for q in range(PARTS)]
        ctx_in = [sb(f"ctx_in{p}", [P, NK, S]) for p in range(2)]
        cT = [sb(f"cT{q}", [P, NK, S], F16) for q in range(PARTS)]
        x_res = [sb(f"x_res{p}", [P, NT, D]) for p in range(2)]
        x_bias = sb("x_bias", [P, NT, D])
        t2 = sb("t2", [P, NT, D])
        t2_b2 = sb("t2_b2", [P, NT, D])
        stats2 = sb("stats2", [P, NT, 6])
        mv2 = sb("mv2", [P, NT, 2])
        var2, rstd2 = sb("var2", [P, NT]), sb("rstd2", [P, NT])
        tg = sb("tg", [P, NT, D])
        tn = sb("tn", [P, NT, D])
        tT = [sb(f"tT{q}", [P, NK, S], F16) for q in range(PARTS)]
        relu32 = sb("relu32", [P, 2, 2, S])
        hid = [sb(f"hid{q}", [P, NF, S], F16) for q in range(PARTS)]
        y = sb("y", [P, NT, D])

        score_bank = [bank(f"score_bank{n}") for n in range(2)]
        turn_bank = [bank(f"turn_bank{n}") for n in range(2)]
        av_bank = bank("av_bank")
        lin = [bank(f"lin{n}") for n in range(3)]

        def halves(t):
            return t[:, :].rearrange("p (h c) -> p h c", h=2)

        v_bank, ot_bank, proj_bank, xt_bank = lin[2], [lin[0], lin[2]], lin[1], lin[0]
        q_bank, on_bank, k_bank, l2t_bank = lin[0], lin[2], lin[0], lin[2]
        f1_bank, f2_bank = [lin[1], lin[0], lin[2], lin[1]], lin[0]
        first_k_bank = lin[1]

        cols_in, eye_in, rows_in, more_rows_in = sem("cols_in"), sem("eye_in"), sem("rows_in"), sem("more_rows_in")
        qkv_in = [sem(f"{n}_in") for n in ("wq", "wk", "wv")]
        og_in, w1_in, w2_in = sem("og_in"), sem("w1_in"), sem("w2_in")
        x_loaded = [sem(f"x_loaded{p}") for p in range(2)]
        mask_loaded = [sem(f"mask_loaded{p}") for p in range(2)]
        ctx_loaded = [sem(f"ctx_loaded{p}") for p in range(2)]
        res_loaded = [sem(f"res_loaded{p}") for p in range(2)]
        q_written, k_written = sem("q_written"), sem("k_written")
        stacked = [sem(f"stacked{p}") for p in range(2)]
        y_free = sem("y_free")
        dve_passed, sp_passed = sem("dve_passed"), sem("sp_passed")
        w_hi_done, w_lo_done = sem("w_hi_done"), sem("w_lo_done")
        bias_done, late_mm, late_done = sem("bias_done"), sem("late_mm"), sem("late_done")
        v_zeroed, q_zeroed, k_zeroed = sem("v_zeroed"), sem("q_zeroed"), sem("k_zeroed")
        half_set, blank_set = sem("half_set"), sem("blank_set")
        st1_done, mv1_done, var1_done, xg_done = sem("st1_done"), sem("mv1_done"), sem("var1_done"), sem("xg_done")
        rstd1_done, xn_done = sem("rstd1_done"), sem("xn_done")
        xt_ready, xt_hi, xt_split = sem("xt_ready"), sem("xt_hi"), sem("xt_split")
        q_ready, q_hi, q_split = sem("q_ready"), sem("q_hi"), sem("q_split")
        k_ready, k_hi, k_split = sem("k_ready"), sem("k_hi"), sem("k_split")
        v_ready, v_copied = sem("v_ready"), sem("v_copied")
        mask_ready = sem("mask_ready")
        scores_ready, max_done, sub_done = sem("scores_ready"), sem("max_done"), sem("sub_done")
        turned, exp_done, av_ready, av_copied = sem("turned"), sem("exp_done"), sem("av_ready"), sem("av_copied")
        ot_ready, recip_done, o_done = sem("ot_ready"), sem("recip_done"), sem("o_done")
        on_ready, on_hi, on_split = sem("on_ready"), sem("on_hi"), sem("on_split")
        ctx_hi, ctx_split, x_bias_done = sem("ctx_hi"), sem("ctx_split"), sem("x_bias_done")
        proj_ready, t2_done, t2_b2_done = sem("proj_ready"), sem("t2_done"), sem("t2_b2_done")
        st2_done, mv2_done, var2_done, tg_done = sem("st2_done"), sem("mv2_done"), sem("var2_done"), sem("tg_done")
        rstd2_done, tn_done = sem("rstd2_done"), sem("tn_done")
        l2t_ready, l2t_hi, l2t_split = sem("l2t_ready"), sem("l2t_hi"), sem("l2t_split")
        f1_ready, f1_hi, f1_relu, f1_split = sem("f1_ready"), sem("f1_hi"), sem("f1_relu"), sem("f1_split")
        f2_ready, y_done = sem("f2_ready"), sem("y_done")

        def nth_of_parity(b, p, each):
            return (b - p) * (each // 2) + each

        def run_steps(eng, step):
            step(0, 0, True, False, False)
            step(0, 1, True, True, False)
            with eng.Fori(1, BATCHES // 2) as j:
                step(j, 0, True, True, True)
                step(j, 1, True, True, True)
            step(BATCHES // 2, 0, False, True, True)
            step(BATCHES // 2, 1, False, False, True)

        def early(i):
            return isinstance(i, int) and i == 1

        def batch(tensor, j, p, back):
            return tensor[j + (p - back) // 2, (p - back) % 2]

        def behind(i, h, lag, has_b, has_c):
            return (i - 1, h - lag, has_b) if h >= lag else (i - 2, HEADS + h - lag, has_c)

        block = stack.enter_context(nc.Block())

        @block.sync
        def _(sp):
            def load_weight(n, w, loaded):
                sp.dma_start(w_raw[:, n, :, :], w.rearrange("(k p) n -> p k n", p=P)).then_inc(loaded, 16)

            sp.dma_start(x_in[0][:, :, :], x_t[0, 0]).then_inc(x_loaded[0], 16)
            sp.dma_start(row[:, 0:FIRST_ROWS, :], rows[0:FIRST_ROWS].partition_broadcast(P)).then_inc(rows_in, 16)
            sp.dma_start(col[:, :], cols).then_inc(cols_in, 16)
            load_weight(WQ, wqT, qkv_in[WQ])
            sp.dma_start(ident[:, :], eye).then_inc(eye_in, 16)
            load_weight(WK, wkT, qkv_in[WK])
            load_weight(WV, wvT, qkv_in[WV])
            sp.dma_start(w1_raw[:, :, :], w1T.rearrange("(k p) n -> p k n", p=P)).then_inc(w1_in, 16)
            sp.dma_start(x_in[1][:, :, :], x_t[0, 1]).then_inc(x_loaded[1], 16)

            def late_loads():
                load_weight(WO, woT, og_in)
                load_weight(WG, wgT, og_in)
                sp.dma_start(row[:, FIRST_ROWS:, :], rows[FIRST_ROWS:].partition_broadcast(P)).then_inc(more_rows_in, 16)
                sp.dma_start(w2_raw[:, :, :], w2T.rearrange("(k p) n -> p k n", p=P)).then_inc(w2_in, 16)

            def step(j, p, has_a, has_b, has_c):
                i = 2 * j + p
                q = 1 - p
                if has_a:
                    if not isinstance(i, int) or i >= 2:
                        sp.wait_ge(xn_done, (i - 1) * NT)
                        sp.sem_inc(sp_passed, 1)
                        sp.dma_start(x_in[p][:, :, :], batch(x_t, j, p, 0)).then_inc(x_loaded[p], 16)
                    if not isinstance(i, int) or i >= 2:
                        sp.wait_ge(mask_ready, i - 1)
                        sp.sem_inc(sp_passed, 1)
                    sp.dma_start(mask_in[p][:, :, :], batch(mask_t, j, p, 0)).then_inc(mask_loaded[p], 16)
                if has_b:
                    sp.dma_start(ctx_in[q][:, :, :], batch(ctx_t, j, p, 1)).then_inc(ctx_loaded[q], 16)
                    sp.dma_start(x_res[q][:, :, :], batch(x_t, j, p, 1)).then_inc(res_loaded[q], 16)
                if isinstance(i, int) and i == 1:
                    late_loads()
                if has_a:
                    if not isinstance(i, int) or i >= 2:
                        sp.wait_ge(stacked[p], nth_of_parity(i - 2, p, 16 * 8))
                        sp.sem_inc(sp_passed, 1)
                        sp.wait_ge(scores_ready, (i - 1) * HEADS)
                        sp.sem_inc(sp_passed, 1)
                    for kind, split, written in ((0, q_split, q_written), (1, k_split, k_written)):
                        sp.wait_ge(split, (i + 1) * NK)
                        sp.sem_inc(sp_passed, 1)
                        sp.dma_start(scratch[p, kind].rearrange("t (k p) s -> p t k s", p=P),
                                     qk_parts[:, kind, :, :, :]).then_inc(written, 16)
                    for kind, written, dst, parts in ((0, q_written, q_stack[p], Q_PARTS),
                                                      (1, k_written, k_stack[p], K_PARTS)):
                        sp.wait_ge(written, (i + 1) * 16)
                        sp.sem_inc(sp_passed, 1)
                        for n, part in enumerate(parts):
                            sp.dma_start(dst[n * HD:(n + 1) * HD, :, :],
                                         scratch[p, kind, part].rearrange("(h r) s -> r h s", r=HD)
                                         ).then_inc(stacked[p], 16)

            run_steps(sp, step)

        @block.tensor
        def _(pe):
            def keep_warm(products, bank_):
                for n in range(products):
                    pe.matmul(bank_[:, 0:D], blank[:, 0:P], blank[:, :], start=True, stop=True)

            def turn(dst, src):
                for k in range(2):
                    for t in range(2):
                        last = pe.transpose(dst[:, k, t * P:(t + 1) * P], src[:, t, k * P:(k + 1) * P],
                                            ident[:, :])
                return last

            def product(dst, left, right, start, stop, open_group=False):
                pairs = ((0, 0), (1, 0), (0, 1))
                for n, (a, b) in enumerate(pairs):
                    last = pe.matmul(dst, left[a], right[b], start=start and n == 0,
                                     stop=stop and n == len(pairs) - 1, skip_group_check=open_group)
                return last

            def output_of_v_bias():
                pe.wait_ge(og_in, 32)
                pe.wait_ge(late_done, 1)
                pe.wait_ge(k_split, 2 * NK)
                for k in range(NK):
                    last = pe.matmul(lin[1][:, 0:D], bv_wide[:, k, :], w_raw[:, WO, k, :],
                                     start=k == 0, stop=k == NK - 1)
                last.then_inc(late_mm, 1)

            def scores(b, h, p):
                if h == 0:
                    pe.wait_ge(stacked[p], nth_of_parity(b, p, 16 * 8))
                if not isinstance(b, int) or b * HEADS + h >= 2:
                    pe.wait_ge(max_done, b * HEADS * NT + (h - 1) * NT)
                for t in range(NT):
                    last = pe.matmul(halves(score_bank[h % 2])[:, t, :], q_stack[p][:, h, t * P:(t + 1) * P],
                                     k_stack[p][:, h, :], start=True, stop=True)
                last.then_inc(scores_ready, 1)

            def turn_scores(b, h):
                pe.wait_ge(sub_done, b * HEADS + h + 1)
                if not isinstance(b, int) or b * HEADS + h >= 2:
                    pe.wait_ge(exp_done, b * HEADS + h - 1)
                turn(halves(turn_bank[h % 2]), masked[:, h % SM_RING, :, :]).then_inc(turned, 1)

            def apply_v(b, g, p):
                if g == 0:
                    pe.wait_ge(v_copied, b + 1)
                pe.wait_ge(exp_done, b * HEADS + (g + 1) * GROUP)
                if not isinstance(b, int) or b * GROUPS + g >= 1:
                    pe.wait_ge(av_copied, b * GROUPS + g)
                for t in range(NT):
                    for j in range(GROUP):
                        h = g * GROUP + j
                        last = pe.matmul(av_bank[j * COLS:(j + 1) * COLS, 0:S], v_cols[p][:, t, h, :],
                                         probsT[:, h % PT_RING, t, :], start=t == 0, stop=t == NT - 1,
                                         skip_group_check=True)
                last.then_inc(av_ready, 1)

            def project(bank_, w):
                for m in range(NK):
                    for k in range(NK):
                        last = product(halves(bank_)[:, m, :],
                                       [t[:, w, k, m * P:(m + 1) * P] for t in (w_hi, w_lo)],
                                       [xT[0][:, k, :], xT[1][:, k, :]], k == 0, k == NK - 1)
                return last

            def turn_normed(b):
                pe.wait_ge(xn_done, (b + 1) * NT)
                turn(halves(xt_bank), xn[:, :, :]).then_inc(xt_ready, 1)

            def project_q(b):
                pe.wait_ge(xt_split, b + 1)
                project(q_bank, WQ).then_inc(q_ready, 1)

            def project_v(bank_):
                for t in range(NT):
                    for k in range(NK):
                        last = product(halves(bank_)[:, t, :], [z[:, k, t * P:(t + 1) * P] for z in xT],
                                       [w_hi[:, WV, k, :], w_lo[:, WV, k, :]], k == 0, k == NK - 1)
                last.then_inc(v_ready, 1)

            def fill_step_0():
                pe.wait_ge(w_lo_done, PARTS_DONE[WV])
                project_v(v_bank)
                keep_warm(WARM_XT, score_bank[0])
                pe.wait_ge(q_split, NK)
                turn_normed(1)
                keep_warm(WARM_Q, score_bank[0])
                project_q(1)
                pe.wait_ge(k_split, NK)
                project(first_k_bank, WK).then_inc(k_ready, 1)
                keep_warm(WARM_SCORES, score_bank[0])

            def step(j, p, has_a, has_b, has_c):
                i = 2 * j + p
                q = 1 - p
                c = i - 2
                if isinstance(i, int) and i == 1:
                    pe.wait_ge(q_zeroed, 1)
                    pe.wait_ge(k_zeroed, 3)
                for h in range(HEADS):
                    if has_b:
                        scores(i - 1, h, q)
                    tb, th, present = behind(i, h, T_LAG, has_b, has_c)
                    if present:
                        turn_scores(tb, th)
                    if h % GROUP == T_LAG % GROUP:
                        tb, th, present = behind(i, h, T_LAG + GROUP, has_b, has_c)
                        if present:
                            apply_v(tb, th // GROUP, q if h >= T_LAG + GROUP else p)
                    if has_a and h == SLOT_V and not (isinstance(i, int) and i == 0):
                        if has_c:
                            pe.wait_ge(on_split, c + 1)
                        else:
                            pe.wait_ge(v_copied, i)
                        project_v(v_bank)
                    if has_c and h in SLOT_OT:
                        u = SLOT_OT.index(h)
                        pe.wait_ge(av_copied, c * GROUPS + 2 * u + 2)
                        if u == 0 and has_b:
                            pe.wait_ge(max_done, (i - 1) * HEADS * NT + NT)
                        elif u == 0:
                            pe.wait_ge(y_done, c)
                        elif has_b:
                            pe.wait_ge(v_copied, i)
                        dst = ot_bank[u][:, :].rearrange("p (t g c) -> p t g c", t=NT, g=2)
                        for g in range(2):
                            for t in range(NT):
                                last = pe.transpose(dst[:, t, g, :],
                                                    oT_wide[:, 2 * u + g, t * P:(t + 1) * P], ident[:, :])
                        last.then_inc(ot_ready, 1)
                    if has_c and h in SLOT_PROJ_CTX:
                        t = SLOT_PROJ_CTX.index(h)
                        if t == 0:
                            pe.wait_ge(w_lo_done, PARTS_DONE[WG])
                            pe.wait_ge(late_done, 3)
                            pe.wait_ge(ctx_split, c + 1)
                        for k in range(NK):
                            product(halves(proj_bank)[:, t, :], [z[:, k, t * P:(t + 1) * P] for z in cT],
                                    [w_hi[:, WG, k, :], w_lo[:, WG, k, :]], t == 0 and k == 0, False,
                                    open_group=True)
                    if has_a and h == SLOT_XT and not early(i):
                        if isinstance(i, int) and i == 0:
                            pe.wait_ge(eye_in, 16)
                        if has_c:
                            pe.wait_ge(o_done, c * 2 + 1)
                        turn_normed(i)
                    if has_c and h == SLOT_ON:
                        if not has_b:
                            keep_warm(WARM_ON, score_bank[0])
                        pe.wait_ge(o_done, (c + 1) * 2)
                        turn(halves(on_bank), o_norm[:, :, :, :].rearrange("p t h d -> p t (h d)")
                             ).then_inc(on_ready, 1)
                    if has_a and h == SLOT_Q and not early(i):
                        if isinstance(i, int) and i == 0:
                            pe.wait_ge(w_lo_done, PARTS_DONE[WQ])
                        project_q(i)
                    if has_c and h == SLOT_PROJ_O:
                        if not has_b:
                            keep_warm(WARM_PO, score_bank[0])
                        pe.wait_ge(on_split, c + 1)
                        for t in range(NT):
                            for k in range(NK):
                                last = product(halves(proj_bank)[:, t, :], [z[:, k, t * P:(t + 1) * P] for z in oT],
                                               [w_hi[:, WO, k, :], w_lo[:, WO, k, :]], False, k == NK - 1,
                                               open_group=True)
                        last.then_inc(proj_ready, 1)
                    if has_a and h == SLOT_K and not early(i):
                        if isinstance(i, int) and i == 0:
                            pe.wait_ge(w_lo_done, PARTS_DONE[WK])
                        else:
                            pe.wait_ge(q_split, (i + 1) * NK)
                        project(first_k_bank if isinstance(i, int) and i == 0 else k_bank, WK).then_inc(k_ready, 1)
                    if has_c and h == SLOT_L2T:
                        if not has_b:
                            keep_warm(WARM_L2T, score_bank[0])
                        if has_a:
                            pe.wait_ge(v_copied, i + 1)
                        pe.wait_ge(tn_done, (c + 1) * NT)
                        turn(halves(l2t_bank), tn[:, :, :]).then_inc(l2t_ready, 1)
                    if has_c and h in SLOT_F1:
                        u = SLOT_F1.index(h)
                        if u == 0:
                            if not has_b:
                                keep_warm(WARM_F1, score_bank[0])
                            pe.wait_ge(w_lo_done, PARTS_DONE[W1])
                            pe.wait_ge(l2t_split, c + 1)
                        if u == 1 and has_a:
                            pe.wait_ge(k_split, (i + 1) * NK)
                        if u == 3:
                            pe.wait_ge(f1_relu, c * NF + 2)
                        for half in range(2):
                            m = 2 * u + half
                            for k in range(NK):
                                last = product(halves(f1_bank[u])[:, half, :],
                                               [w[:, k, m * P:(m + 1) * P] for w in (w1_hi, w1_lo)],
                                               [tT[0][:, k, :], tT[1][:, k, :]], k == 0, k == NK - 1)
                        last.then_inc(f1_ready, 1)
                    if has_c and h in SLOT_F2:
                        for u in SLOT_F2[h]:
                            pe.wait_ge(f1_split, c * UNITS + u + 1)
                            if u == 0:
                                pe.wait_ge(w_lo_done, PARTS_DONE[W2])
                            if u == 0:
                                pe.wait_ge(f1_relu, c * NF + 4)
                            for t in range(NT):
                                for k in (2 * u, 2 * u + 1):
                                    last = product(halves(f2_bank)[:, t, :], [z[:, k, t * P:(t + 1) * P] for z in hid],
                                                   [w2_hi[:, k, :], w2_lo[:, k, :]],
                                                   k == 0 and t == 0, k == NF - 1, open_group=True)
                            if u == UNITS - 1:
                                last.then_inc(f2_ready, 1)
                if isinstance(i, int) and i == 0:
                    fill_step_0()
                if isinstance(i, int) and i == 1:
                    output_of_v_bias()

            pe.wait_ge(blank_set, 1)
            keep_warm(WARM_UP, score_bank[0])
            run_steps(pe, step)

        @block.scalar
        def _(act):
            act.sem_inc(y_free, 16)

            def copy_v(b, p, bank_):
                act.wait_ge(v_ready, b + 1)
                if isinstance(b, int) and b == 0:
                    act.wait_ge(v_zeroed, 4)
                act.copy(v_cols[p][:, :, :, 0:HD],
                         halves(bank_).rearrange("p t (h d) -> p t h d", d=HD)).then_inc(v_copied, 1)

            def high_normed(b):
                act.wait_ge(xt_ready, b + 1)
                act.copy(xT[0][:, :, :], halves(xt_bank)).then_inc(xt_hi, 1)

            def high_qk(b, kind, bank_):
                act.wait_ge((q_ready, k_ready)[kind], b + 1)
                if isinstance(b, int) and b == 0:
                    act.wait_ge(bias_done, 1)
                else:
                    act.wait_ge((q_written, k_written)[kind], b * 16)
                for m in range(NK):
                    bias = (bias_q[:, m:m + 1], col[:, C_BK + m:C_BK + m + 1])[kind]
                    act.activation(qk_parts[:, kind, 0, m, :], halves(bank_)[:, m, :],
                                   ACT.Identity, bias=bias).then_inc((q_hi, k_hi)[kind], 1)

            def high_weight(w):
                act.wait_ge(qkv_in[w], 16)
                act.activation(w_hi[:, w, :, :], w_raw[:, w, :, :], ACT.Copy,
                               scale=SCALE if w == WQ else 1.0).then_inc(w_hi_done, 1)

            for w in (WQ, WK):
                high_weight(w)

            def fill_step_0():
                copy_v(0, 0, v_bank)
                act.wait_ge(w1_in, 16)
                for tiles in W1_PIECES:
                    act.copy(w1_hi[:, tiles, :], w1_raw[:, tiles, :]).then_inc(w_hi_done, 1)
                high_normed(1)
                high_qk(1, 0, q_bank)
                high_qk(1, 1, first_k_bank)

            def later_weights(h):
                if h in SLOT_OG_PARTS:
                    w = (WO, WG)[SLOT_OG_PARTS.index(h)]
                    act.wait_ge(og_in, 32)
                    act.copy(w_hi[:, w, :, :], w_raw[:, w, :, :]).then_inc(w_hi_done, 1)
                if h in SLOT_W2_PARTS:
                    tiles = W2_PIECES[SLOT_W2_PARTS.index(h)]
                    act.wait_ge(w2_in, 16)
                    act.copy(w2_hi[:, tiles, :], w2_raw[:, tiles, :]).then_inc(w_hi_done, 1)

            def step(j, p, has_a, has_b, has_c):
                i = 2 * j + p
                q = 1 - p
                c = i - 2
                for h in range(HEADS):
                    tb, th, present = behind(i, h, T_LAG, has_b, has_c)
                    if present:
                        act.wait_ge(turned, tb * HEADS + th + 1)
                        if not isinstance(tb, int) or tb * HEADS + th >= PT_RING:
                            act.wait_ge(av_ready, tb * GROUPS + th // GROUP - 1)
                        act.activation(probsT[:, th % PT_RING, :, :], halves(turn_bank[th % 2]),
                                       ACT.Exp).then_inc(exp_done, 1)
                    if h % GROUP == T_LAG % GROUP:
                        tb, th, present = behind(i, h, T_LAG + GROUP, has_b, has_c)
                        if present:
                            g = th // GROUP
                            act.wait_ge(av_ready, tb * GROUPS + g + 1)
                            act.copy(oT_wide[:, g, :], av_bank[:, 0:S]).then_inc(av_copied, 1)
                    if has_c and h == SLOT_ON:
                        act.wait_ge(on_ready, c + 1)
                        act.copy(oT[0][:, :, :], halves(on_bank)).then_inc(on_hi, 1)
                    if has_a and h == SLOT_XT and not early(i):
                        high_normed(i)
                        if isinstance(i, int) and i == 0:
                            high_weight(WV)
                    if has_a and h == SLOT_Q and not early(i):
                        high_qk(i, 0, q_bank)
                    if has_a and h == SLOT_K and not early(i):
                        high_qk(i, 1, first_k_bank if isinstance(i, int) and i == 0 else k_bank)
                    if has_c and h == SLOT_L2T:
                        act.wait_ge(l2t_ready, c + 1)
                        act.copy(tT[0][:, :, :], halves(l2t_bank)).then_inc(l2t_hi, 1)
                    if has_c and h in SLOT_F1:
                        u = SLOT_F1.index(h)
                        act.wait_ge(f1_ready, c * UNITS + u + 1)
                        if u >= 2:
                            act.wait_ge(f1_split, c * UNITS + u - 1)
                        for half in range(2):
                            m = 2 * u + half
                            act.activation(relu32[:, u % 2, half, :], halves(f1_bank[u])[:, half, :], ACT.Relu,
                                           bias=col[:, C_B1 + m:C_B1 + m + 1]).then_inc(f1_relu, 1)
                        act.wait_ge(f1_relu, c * NF + 2 * u + 2)
                        act.copy(hid[0][:, 2 * u:2 * u + 2, :], relu32[:, u % 2, :, :]).then_inc(f1_hi, 1)
                    if has_b and h == SLOT_CTX:
                        act.wait_ge(ctx_loaded[q], nth_of_parity(i - 1, q, 16))
                        act.copy(cT[0][:, :, :], ctx_in[q][:, :, :]).then_inc(ctx_hi, 1)
                    if has_a and h == SLOT_V and not (isinstance(i, int) and i == 0):
                        copy_v(i, p, v_bank)
                    if isinstance(i, int) and i == 1:
                        later_weights(h)
                if isinstance(i, int) and i == 0:
                    fill_step_0()
                if has_c:
                    act.wait_ge(y_done, c + 1)
                    act.dma_start(batch(out_t, j, p, 2), y[:, :, :]).then_inc(y_free, 16)

            run_steps(act, step)
            act.wait_ge(y_free, (BATCHES + 1) * 16)

        @block.vector
        def _(dve):
            def moments(src, stats, mv, var, sems, b):
                st_done, mv_done, var_done = sems
                for t in range(NT):
                    dve.bn_stats(stats[:, t, :], src[:, t, :]).then_inc(st_done, 1)
                for t in range(NT):
                    dve.wait_ge(st_done, b * NT + t + 1)
                    dve.sem_inc(dve_passed, 1)
                    dve.bn_aggr(mv[:, t, :], stats[:, t, :]).then_inc(mv_done, 1)
                dve.wait_ge(mv_done, (b + 1) * NT)
                dve.tensor_scalar(var[:, :], mv[:, :, 1], EPS, None, ALU.add).then_inc(var_done, 1)

            def center(src, mv, gain, between, between_done):
                for t in range(NT):
                    dve.scalar_tensor_tensor(between[:, t, :], src[:, t, :], mv[:, t, 0:1], row[:, gain, :],
                                             ALU.subtract, ALU.mult).then_inc(between_done, 1)

            def normalize(between, rstd, shift, dst, rstd_done, between_done, done, b):
                dve.wait_ge(rstd_done, b + 1)
                for t in range(NT):
                    dve.wait_ge(between_done, b * NT + t + 1)
                    dve.scalar_tensor_tensor(dst[:, t, :], between[:, t, :], rstd[:, t:t + 1], row[:, shift, :],
                                             ALU.mult, ALU.add).then_inc(done, 1)

            def moments1(b, p):
                moments(x_in[p], stats1, mv1, var1, (st1_done, mv1_done, var1_done), b)

            def normalize1(b, p):
                center(x_in[p], mv1, R_G1, xg, xg_done)
                normalize(xg, rstd1, R_BE1, xn, rstd1_done, xg_done, xn_done, b)

            dve.memset(blank[:, :], 0.0).then_inc(blank_set, 1)
            dve.memset(q_stack[0][len(Q_PARTS) * HD:STACK, :, :], 0.0).then_inc(q_zeroed, 1)
            dve.wait_ge(x_loaded[0], 16)
            moments1(0, 0)
            dve.wait_ge(rows_in, 16)
            normalize1(0, 0)
            dve.wait_ge(cols_in, 16)
            dve.tensor_scalar(bias_q[:, :], col[:, C_BQ:C_BQ + NK], SCALE, None, ALU.mult).then_inc(bias_done, 1)

            def low_weight(w):
                dve.wait_ge(w_hi_done, PARTS_DONE[w])
                dve.scalar_tensor_tensor(w_lo[:, w, :, :], w_raw[:, w, :, :], SCALE if w == WQ else 1.0,
                                         w_hi[:, w, :, :], ALU.mult, ALU.subtract).then_inc(w_lo_done, 1)

            low_weight(WQ)

            def fill_step_0():
                dve.wait_ge(xt_ready, 1)
                normalize1(1, 1)
                bias_of_mask(0, 0)
                dve.tensor_copy(bv_wide[:, :, :], col[:, C_BV:C_BV + NK].unsqueeze(2).to_broadcast([P, NK, P])
                                ).then_inc(late_done, 1)
                low_normed(1)
                for n, tiles in enumerate(W1_PIECES):
                    dve.wait_ge(w_hi_done, PARTS_DONE[W1] - len(W1_PIECES) + n + 1)
                    dve.tensor_tensor(w1_lo[:, tiles, :], w1_raw[:, tiles, :], w1_hi[:, tiles, :],
                                      ALU.subtract).then_inc(w_lo_done, 1)
                low_qk(1, 0, q_bank)

            def low_normed(b):
                low_part(xT[1][:, :, :], xt_bank, xT[0][:, :, :], xt_hi, b + 1, xt_split)

            def low_qk(b, kind, bank_):
                dve.wait_ge((q_hi, k_hi)[kind], (b + 1) * NK)
                for m in range(NK):
                    bias = (bias_q[:, m:m + 1], col[:, C_BK + m:C_BK + m + 1])[kind]
                    dve.scalar_tensor_tensor(qk_parts[:, kind, 1, m, :], halves(bank_)[:, m, :], bias,
                                             qk_parts[:, kind, 0, m, :],
                                             ALU.add, ALU.subtract).then_inc((q_split, k_split)[kind], 1)

            def bias_of_mask(b, p):
                dve.wait_ge(mask_loaded[p], nth_of_parity(b, p, 16))
                dve.tensor_scalar(mask_bias[p][:, :, :], mask_in[p][:, :, :], 1.0, MASKED,
                                  ALU.subtract, ALU.mult).then_inc(mask_ready, 1)

            def later_low_parts(s):
                if s in SLOT_OG_PARTS:
                    low_weight((WO, WG)[SLOT_OG_PARTS.index(s)])
                if s in SLOT_W2_PARTS:
                    n = SLOT_W2_PARTS.index(s)
                    tiles = W2_PIECES[n]
                    dve.wait_ge(w_hi_done, PARTS_DONE[W2] - len(W2_PIECES) + n + 1)
                    dve.tensor_tensor(w2_lo[:, tiles, :], w2_raw[:, tiles, :], w2_hi[:, tiles, :],
                                      ALU.subtract).then_inc(w_lo_done, 1)

            def residual_bias():
                dve.wait_ge(more_rows_in, 16)
                dve.tensor_tensor(bog[:, :], row[:, R_BO, :], row[:, R_BG, :], ALU.add).then_inc(late_done, 1)
                dve.wait_ge(late_done, 2)
                dve.wait_ge(late_mm, 1)
                dve.tensor_tensor(bias_t2[:, :], lin[1][:, 0:D], bog[:, :], ALU.add).then_inc(late_done, 1)

            def low_part(dst, bank_, hi, hi_sem, count, split):
                dve.wait_ge(hi_sem, count)
                dve.tensor_tensor(dst, halves(bank_), hi, ALU.subtract).then_inc(split, 1)

            def step(j, p, has_a, has_b, has_c):
                i = 2 * j + p
                q = 1 - p
                c = i - 2
                for h in range(HEADS + 1):
                    s = h - 1
                    if has_c and s in SLOT_OT:
                        u = SLOT_OT.index(s)
                        wide = ot_bank[u][:, :].rearrange("p (t h c) -> p t h c", t=NT, c=COLS)
                        heads = slice(u * HEADS // 2, (u + 1) * HEADS // 2)
                        dve.wait_ge(ot_ready, c * 2 + u + 1)
                        dve.reciprocal(recip[:, :, heads], wide[:, :, :, HD]).then_inc(recip_done, 1)
                        dve.wait_ge(recip_done, c * 2 + u + 1)
                        dve.tensor_tensor(o_norm[:, :, heads, :], wide[:, :, :, 0:HD],
                                          recip[:, :, heads].unsqueeze(3).to_broadcast([P, NT, HEADS // 2, HD]),
                                          ALU.mult).then_inc(o_done, 1)
                    if has_c and s == SLOT_ON:
                        low_part(oT[1][:, :, :], on_bank, oT[0][:, :, :], on_hi, c + 1, on_split)
                    if has_a and s == SLOT_XT and not early(i):
                        low_normed(i)
                        if isinstance(i, int) and i == 0:
                            low_weight(WK)
                            low_weight(WV)
                    if has_a and s == SLOT_Q_LOW and not early(i):
                        low_qk(i, 0, q_bank)
                    if isinstance(i, int) and i == 0 and s == SLOT_Q_LOW:
                        dve.wait_ge(x_loaded[1], 16)
                        dve.wait_ge(xn_done, NT)
                        moments1(1, 1)
                    if has_a and s == SLOT_K_LOW and not early(i):
                        low_qk(i, 1, first_k_bank if isinstance(i, int) and i == 0 else k_bank)
                    if has_c and s == SLOT_L2T:
                        low_part(tT[1][:, :, :], l2t_bank, tT[0][:, :, :], l2t_hi, c + 1, l2t_split)
                    if has_c and s in SLOT_F1:
                        u = SLOT_F1.index(s)
                        dve.wait_ge(f1_hi, c * UNITS + u + 1)
                        dve.tensor_tensor(hid[1][:, 2 * u:2 * u + 2, :], relu32[:, u % 2, :, :],
                                          hid[0][:, 2 * u:2 * u + 2, :], ALU.subtract).then_inc(f1_split, 1)
                    if has_b and s == SLOT_CTX:
                        dve.wait_ge(ctx_hi, i)
                        dve.tensor_tensor(cT[1][:, :, :], ctx_in[q][:, :, :], cT[0][:, :, :],
                                          ALU.subtract).then_inc(ctx_split, 1)
                    if h < HEADS and has_b:
                        b = i - 1
                        ring = h % SM_RING
                        dve.wait_ge(scores_ready, b * HEADS + h + 1)
                        if h == 0:
                            dve.wait_ge(mask_ready, b + 1)
                        if not isinstance(b, int) or b * HEADS + h >= SM_RING:
                            dve.wait_ge(turned, b * HEADS + h + 1 - SM_RING)
                        dve.sem_inc(dve_passed, 1)
                        for t in range(NT):
                            dve.tensor_tensor_reduce(masked[:, ring, t, :], halves(score_bank[h % 2])[:, t, :],
                                                     mask_bias[q][:, t, :], 1.0, LOWEST, ALU.add, ALU.max,
                                                     top[:, ring, t:t + 1]).then_inc(max_done, 1)
                    if has_c and h == SLOT_T2:
                        dve.wait_ge(proj_ready, c + 1)
                        dve.wait_ge(x_bias_done, c + 1)
                        dve.tensor_tensor(t2[:, :, :], halves(proj_bank), x_bias[:, :, :],
                                          ALU.add).then_inc(t2_done, 1)
                        dve.wait_ge(t2_done, c + 1)
                        moments(t2, stats2, mv2, var2, (st2_done, mv2_done, var2_done), c)
                    if has_c and h == SLOT_TG:
                        center(t2, mv2, R_G2, tg, tg_done)
                    if has_c and h == SLOT_LN2:
                        normalize(tg, rstd2, R_BE2, tn, rstd2_done, tg_done, tn_done, c)
                    if has_a and h == SLOT_LN1 and not isinstance(i, int):
                        dve.wait_ge(x_loaded[p], nth_of_parity(i, p, 16))
                        moments1(i, p)
                    if has_a and h == SLOT_XN and not isinstance(i, int):
                        dve.wait_ge(xt_ready, i)
                        normalize1(i, p)
                    if has_a and h == SLOT_MASK and not (isinstance(i, int) and i == 0):
                        bias_of_mask(i, p)
                    if early(i):
                        if s == SLOT_LATE_K:
                            low_qk(1, 1, first_k_bank)
                        later_low_parts(s)
                if has_c:
                    dve.wait_ge(f2_ready, c + 1)
                    dve.wait_ge(t2_b2_done, c + 1)
                    dve.wait_ge(y_free, (c + 1) * 16)
                    dve.tensor_tensor(y[:, :, :], halves(f2_bank), t2_b2[:, :, :], ALU.add).then_inc(y_done, 1)
                if isinstance(i, int) and i == 0:
                    fill_step_0()
                if isinstance(i, int) and i == 1:
                    residual_bias()

            run_steps(dve, step)

        @block.gpsimd
        def _(pool):
            pool.memset(minus_half[:, :], -0.5).then_inc(half_set, 1)

            def inverse_root(rstd, var, var_done, rstd_done, b):
                pool.wait_ge(var_done, b + 1)
                pool.tensor_tensor(rstd[:, :], var[:, :], minus_half[:, :], ALU.pow).then_inc(rstd_done, 1)

            pool.wait_ge(half_set, 1)

            def zero_rows(t):
                pool.memset(t[len(Q_PARTS) * HD:STACK, :, :], 0.0).then_inc(k_zeroed, 1)

            zero_rows(k_stack[0])
            pool.wait_ge(k_zeroed, 1)
            inverse_root(rstd1, var1, var1_done, rstd1_done, 0)
            for p in range(2):
                pool.memset(v_cols[p][:, :, :, HD:HD + 1], 1.0).then_inc(v_zeroed, 1)
                pool.memset(v_cols[p][:, :, :, HD + 1:COLS], 0.0).then_inc(v_zeroed, 1)
            pool.wait_ge(v_zeroed, 4)
            zero_rows(q_stack[1])
            zero_rows(k_stack[1])
            pool.wait_ge(k_zeroed, 3)

            def rows_over_tiles(r):
                return r.unsqueeze(1).to_broadcast([P, NT, D])

            def step(j, p, has_a, has_b, has_c):
                i = 2 * j + p
                c = i - 2
                for h in range(HEADS):
                    sb_, sh, present = behind(i, h, 1, has_b, has_c)
                    if present:
                        ring = sh % SM_RING
                        pool.wait_ge(max_done, (sb_ * HEADS + sh + 1) * NT)
                        pool.tensor_tensor(masked[:, ring, :, :], masked[:, ring, :, :],
                                           top[:, ring, :].unsqueeze(2).to_broadcast([P, NT, S]),
                                           ALU.subtract).then_inc(sub_done, 1)
                    if has_c and h == SLOT_X_BIAS:
                        pool.wait_ge(res_loaded[p], nth_of_parity(c, p, 16))
                        pool.wait_ge(late_done, 3)
                        pool.tensor_tensor(x_bias[:, :, :], x_res[p][:, :, :], rows_over_tiles(bias_t2[:, :]),
                                           ALU.add).then_inc(x_bias_done, 1)
                    if has_a and h == SLOT_ROOT1 and not isinstance(i, int):
                        inverse_root(rstd1, var1, var1_done, rstd1_done, i)
                    if has_c and h == SLOT_ROOT2:
                        inverse_root(rstd2, var2, var2_done, rstd2_done, c)
                    if has_c and h == SLOT_T2_B2:
                        pool.wait_ge(t2_done, c + 1)
                        pool.tensor_tensor(t2_b2[:, :, :], t2[:, :, :], rows_over_tiles(row[:, R_B2, :]),
                                           ALU.add).then_inc(t2_b2_done, 1)
                if isinstance(i, int) and i == 0:
                    inverse_root(rstd1, var1, var1_done, rstd1_done, 1)

            run_steps(pool, step)


def kernel(**inputs):
    import numpy as np
    import concourse.bacc as bacc
    from concourse.bass_utils import run_bass_kernel_spmd

    a = {k.replace("L0_xattn_", ""): np.asarray(v) for k, v in inputs.items()}

    def columns(v):
        return v.reshape(-1, P).T

    arrays = {
        "x": a["x"],
        "ctxT": a["ctx_1024"].transpose(0, 2, 1),
        "mask": a["mask_BxSxS2_fk0"],
        "WqT": a["Wq"].T, "WkT": a["Wk"].T, "WvT": a["Wv"].T, "WoT": a["Wo"].T, "WgT": a["Wg"].T,
        "W1T": a["W1"].T, "W2T": a["W2"].T,
        "cols": np.concatenate([columns(a[n]) for n in ("bq", "bk", "bv", "b1")], axis=1),
        "rows": np.stack([a[n] for n in ("g1", "be1", "g2", "be2", "bo", "bg", "b2")]),
        "eye": np.eye(P, dtype=np.float32),
    }
    arrays = {f"in_{k}": np.ascontiguousarray(v) for k, v in arrays.items()}
    nc = bacc.Bacc("TRN2", target_bir_lowering=False, num_devices=1)
    args = [nc.dram_tensor(k, v.shape, mybir.dt.from_np(v.dtype), kind="ExternalInput").ap()
            for k, v in arrays.items()]
    args.append(nc.dram_tensor("out", (BATCHES, S, D), F32, kind="ExternalOutput").ap())
    build(nc, *args)
    r = run_bass_kernel_spmd(nc, [arrays], core_ids=[0])
    return r.results[0]["out"]
```
